# Optimizing a Trainium2 kernel written in Bass

```python
import numpy as np
import jax
import jax.numpy as jnp

def _softmax(x, axis=-1):
    return jax.nn.softmax(x, axis=axis)

def _gelu(x):
    return jax.nn.gelu(x, approximate=True)

def _silu(x):
    return jax.nn.silu(x)

def _sigmoid(x):
    return jax.nn.sigmoid(x)

def _layernorm(x, axis=-1, eps=1e-05):
    m = jnp.mean(x, axis=axis, keepdims=True)
    v = jnp.var(x, axis=axis, keepdims=True)
    return (x - m) / jnp.sqrt(v + eps)

def _scatter_add(tgt, idx, src, axis=0):
    return tgt.at[idx].add(src)

def _segment_sum(src, seg, n):
    return jax.ops.segment_sum(src, seg, n)
kernel_name = 'mk_macaron_d1_jaxref_r4_a7f883'

def setup_inputs(seed: int=0):
    np.random.seed(seed)
    _w = jnp.asarray

    def _L0_attn_setup():
        import jax, jax.numpy as jnp
        import numpy as np
        HEADS = 16
        EPS = 1e-08

        def _attention(x, Wq, Wkv, Wo, heads=HEADS, causal=True, eps=EPS):
            B, N, D = x.shape
            dh = D // heads
            q = x @ Wq.T
            k, v = jnp.split(x @ Wkv.T, 2, axis=-1)

            def split_heads(t):
                return t.reshape(B, N, heads, dh).transpose(0, 2, 1, 3)
            q, k, v = map(split_heads, (q, k, v))
            q = q * dh ** (-0.5)
            sim = jnp.einsum('bhid,bhjd->bhij', q, k)
            mask_value = -jnp.finfo(sim.dtype).max
            if causal:
                causal_mask = jnp.triu(jnp.ones((N, N), dtype=bool), 1)
                sim = jnp.where(causal_mask, mask_value, sim)
            m = jax.lax.stop_gradient(jnp.max(sim, axis=-1, keepdims=True))
            e = jnp.exp(sim - m)
            num = jnp.einsum('bhij,bhjd->bhid', e, v)
            den = jnp.sum(e, axis=-1, keepdims=True) + eps
            out = num / den
            out = out.transpose(0, 2, 1, 3).reshape(B, N, D)
            return out @ Wo.T
        key = jax.random.key(seed)
        k0, k1, k2, k3 = jax.random.split(key, 4)
        B, N, D = (2, 512, 256)
        x = jax.random.normal(k0, (B, N, D), jnp.float32)
        Wq = jax.random.normal(k1, (D, D), jnp.float32) * 0.02
        Wkv = jax.random.normal(k2, (2 * D, D), jnp.float32) * 0.02
        Wo = jax.random.normal(k3, (D, D), jnp.float32) * 0.02
        return {'x': x, 'Wq': Wq, 'Wkv': Wkv, 'Wo': Wo}
    _L0_attn_in = _L0_attn_setup()

    def _L0_ffn_setup():
        import jax, jax.numpy as jnp
        import numpy as np
        H = 256
        E = 8
        B, S = (4, 512)
        key = jax.random.key(seed)
        k1, k2, k3, k4 = jax.random.split(key, 4)
        x = jax.random.normal(k1, (B, S, H), dtype=jnp.float32)
        wg = jax.random.normal(k2, (H, E), dtype=jnp.float32) * 0.02
        W = jax.random.normal(k3, (E, H, H), dtype=jnp.float32) * 0.02
        b = jax.random.normal(k4, (E, H), dtype=jnp.float32) * 0.02
        return {'x': x, 'wg': wg, 'W': W, 'b': b}
    _L0_ffn_in = _L0_ffn_setup()
    _d = {'L0_attn_x': _L0_attn_in['x'], 'L0_attn_Wq': _L0_attn_in['Wq'], 'L0_attn_Wkv': _L0_attn_in['Wkv'], 'L0_attn_Wo': _L0_attn_in['Wo'], 'L0_ffn_wg': _L0_ffn_in['wg'], 'L0_ffn_W': _L0_ffn_in['W'], 'L0_ffn_b': _L0_ffn_in['b']}
    _x0 = _d['L0_attn_x']
    _d['L0_attn_x'] = jax.random.normal(jax.random.fold_in(jax.random.key(seed), 1), (2, 2048, 256), dtype=_x0.dtype)
    del _x0
    return _d

def reference(L0_attn_x, L0_attn_Wq, L0_attn_Wkv, L0_attn_Wo, L0_ffn_wg, L0_ffn_W, L0_ffn_b):

    def _L0_attn_ref(x, Wq, Wkv, Wo):
        import jax, jax.numpy as jnp
        import numpy as np
        HEADS = 16
        EPS = 1e-08

        def _attention(x, Wq, Wkv, Wo, heads=HEADS, causal=True, eps=EPS):
            B, N, D = x.shape
            dh = D // heads
            q = x @ Wq.T
            k, v = jnp.split(x @ Wkv.T, 2, axis=-1)

            def split_heads(t):
                return t.reshape(B, N, heads, dh).transpose(0, 2, 1, 3)
            q, k, v = map(split_heads, (q, k, v))
            q = q * dh ** (-0.5)
            sim = jnp.einsum('bhid,bhjd->bhij', q, k)
            mask_value = -jnp.finfo(sim.dtype).max
            if causal:
                causal_mask = jnp.triu(jnp.ones((N, N), dtype=bool), 1)
                sim = jnp.where(causal_mask, mask_value, sim)
            m = jax.lax.stop_gradient(jnp.max(sim, axis=-1, keepdims=True))
            e = jnp.exp(sim - m)
            num = jnp.einsum('bhij,bhjd->bhid', e, v)
            den = jnp.sum(e, axis=-1, keepdims=True) + eps
            out = num / den
            out = out.transpose(0, 2, 1, 3).reshape(B, N, D)
            return out @ Wo.T
        return _attention(x, Wq, Wkv, Wo)

    def _L0_ffn_ref(x, wg, W, b):
        import jax, jax.numpy as jnp
        import numpy as np
        H = 256
        E = 8
        B, S = (4, 512)
        Bb, Ss, Hh = x.shape
        Ee = wg.shape[1]
        T = Bb * Ss
        C = T // Ee
        xt = x.reshape(T, Hh)
        logits = xt @ wg
        probs = jax.nn.softmax(logits, axis=-1)
        idx = jnp.argmax(probs, axis=-1)
        mask = jax.nn.one_hot(idx, Ee, dtype=xt.dtype)
        locations = jnp.cumsum(mask, axis=0) - mask
        mask = mask * (locations < C).astype(xt.dtype)
        gate = jnp.sum(probs * mask, axis=-1)
        loc_s = jnp.sum(locations * mask, axis=-1).astype(jnp.int32)
        loc_oh = jax.nn.one_hot(loc_s, C, dtype=xt.dtype)
        dispatch = mask[:, :, None] * loc_oh[:, None, :]
        combine = gate[:, None, None] * dispatch
        exp_in = jnp.einsum('tec,th->ech', dispatch, xt)
        exp_out = jnp.einsum('ech,efh->ecf', exp_in, W) + b[:, None, :]
        out = jnp.einsum('tec,ecf->tf', combine, exp_out)
        return out.reshape(Bb, Ss, Hh)
    x = L0_attn_x
    x = x + 0.5 * _L0_ffn_ref(_layernorm(x, axis=-1), L0_ffn_wg, L0_ffn_W, L0_ffn_b)
    x = x + _L0_attn_ref(_layernorm(x, axis=-1), L0_attn_Wq, L0_attn_Wkv, L0_attn_Wo)
    x = x + 0.5 * _L0_ffn_ref(_layernorm(x, axis=-1), L0_ffn_wg, L0_ffn_W, L0_ffn_b)
    return x

_drawn_inputs = setup_inputs


def setup_inputs(seed=0):
    import zlib

    import numpy as np

    out = dict(_drawn_inputs(seed))
    spreads = {}
    factors = {'L0_attn_Wq': 8.0, 'L0_attn_Wkv': 8.0, 'L0_attn_Wo': 8.0, 'L0_ffn_b': 8.0}
    for name, (base, spread) in spreads.items():
        noise = np.random.default_rng([zlib.crc32(name.encode()), seed]).standard_normal(out[name].shape)
        drawn = base * np.exp(spread * noise) if base else spread * noise
        out[name] = jnp.asarray(drawn.astype(out[name].dtype))
    for name, factor in factors.items():
        out[name] = (out[name] * factor).astype(out[name].dtype)
    return out
```

```python
from contextlib import ExitStack

import concourse.bass as bass
from concourse import mybir

P = 128
BATCH, SEQ, D = 2, 2048, 256
HEADS, EXPERTS = 16, 8
DH = D // HEADS
TOKENS = BATCH * SEQ
TILES = TOKENS // P
CAP = TOKENS // EXPERTS
KC = D // P
BT = 4
BLOCK = BT * P
BLOCKS = TOKENS // BLOCK
LN_EPS = 1e-5
DEN_EPS = 1e-8
SCALE = DH ** -0.5
NEG = -3.0e38

GH = 4
GROUPS = BATCH * HEADS // GH
GF = GH * DH
PARTS = 3
ROWS = 6 * DH
AROWS = ROWS + PARTS
WIN = 512
WINS = SEQ // WIN
QT = SEQ // P
UNITS = [(w, kb) for w in range(WINS) for kb in range((w + 1) * WIN // P)]
NU = len(UNITS)
ERING = 4
CHUNKS = [(t, h, c, min(WIN, (t + 1) * P - c * WIN))
          for t in range(QT) for h in range(GH) for c in range(t // BT + 1)]
NC_ = len(CHUNKS)
EARLY_T = 12
EARLY_CHUNKS = sum(1 for c in CHUNKS if c[0] < EARLY_T)
AUX_USES = 6

ALU = mybir.AluOpType
ACT = mybir.ActivationFunctionType
AX = mybir.AxisListType
F32 = mybir.dt.float32
BF16 = mybir.dt.bfloat16
I32 = mybir.dt.int32
ds = bass.ds


class Core:
    pass


def sems(nc, stack, *names):
    return [stack.enter_context(nc.semaphore(n)) for n in names]


def in_pairs(eng, count, body):
    for s in range(2):
        body(0, s)
    with eng.Fori(1, count // 2) as k:
        for s in range(2):
            body(k, s)


def wait_free(eng, sem, value):
    if not isinstance(value, int) or value:
        eng.wait_ge(sem, value)


def wait_alone(eng, sem, value, passed):
    eng.wait_ge(sem, value)
    eng.sem_inc(passed, 1)


def constants(nc, m, io):
    with ExitStack() as st:
        zeros = st.enter_context(nc.sbuf_tensor("zeros", [P, 2048], F32))
        made, zeroed, stored, ones_made, loaded = sems(
            nc, st, "c_made", "c_zeroed", "c_stored", "c_ones", "c_loaded")
        block = st.enter_context(nc.Block())

        @block.sync
        def _(sp):
            sp.dma_start(m.X[:, :, :], io["x"].rearrange("(i p) d -> p i d", p=P)).then_inc(loaded, 16)
            sp.wait_ge(zeroed, 1)
            for xs in m.XS:
                for k in range(TOKENS * D // (P * 2048)):
                    sp.dma_start(xs[k * 1024:(k + 1) * 1024, :].rearrange("(p a) d -> p (a d)", p=P),
                                 zeros[:, :]).then_inc(stored, 16)
            sp.wait_ge(loaded, 16)
            sp.wait_ge(stored, 2 * 4 * 16)

        @block.vector
        def _(dve):
            nc.vector.memset(zeros[:, :], 0.0).then_inc(zeroed, 1)
            nc.vector.memset(m.ones_b[:, :], 1.0).then_inc(ones_made, 1)
            nc.vector.memset(m.neghalf[:, :], -0.5).then_inc(ones_made, 1)

        @block.gpsimd
        def _(pool):
            nc.gpsimd.memset(m.ident_f[:, :], 0.0).then_inc(made, 1)
            nc.gpsimd.memset(m.ident_b[:, :], 0.0).then_inc(made, 1)
            nc.gpsimd.memset(m.before[:, :], 1.0).then_inc(made, 1)
            nc.gpsimd.memset(m.maskneg[:, :], 0.0).then_inc(made, 1)
            pool.wait_ge(made, 4)
            nc.gpsimd.affine_select(out=m.ident_f[:, :], in_=m.ident_f[:, :], compare_op=ALU.not_equal, fill=1.0,
                                    base=0, pattern=[[-1, P]], channel_multiplier=1).then_inc(made, 1)
            nc.gpsimd.affine_select(out=m.ident_b[:, :], in_=m.ident_b[:, :], compare_op=ALU.not_equal, fill=1.0,
                                    base=0, pattern=[[-1, P]], channel_multiplier=1).then_inc(made, 1)
            nc.gpsimd.affine_select(out=m.before[:, :], in_=m.before[:, :], compare_op=ALU.is_gt, fill=0.0,
                                    base=0, pattern=[[1, P]], channel_multiplier=-1).then_inc(made, 1)
            nc.gpsimd.affine_select(out=m.maskneg[:, :], in_=m.maskneg[:, :], compare_op=ALU.is_ge, fill=NEG,
                                    base=WIN - P, pattern=[[-1, WIN]], channel_multiplier=1).then_inc(made, 1)
            for e in range(EXPERTS):
                nc.gpsimd.memset(m.rank[:, :, e:e + 1], float(EXPERTS - e)).then_inc(made, 1)


class Moments:

    def __init__(self, nc, stack, tag, m):
        def sb(name, shape):
            return stack.enter_context(nc.sbuf_tensor(f"{tag}_{name}", shape, F32))

        self.nc, self.m = nc, m
        self.stats = sb("stats", [P, TILES, 6])
        self.work = sb("work", [P, 4, TILES])
        self.mean, self.var_eps, self.rstd = (sb(n, [P, TILES]) for n in ("mean", "var_eps", "rstd"))
        self.st_done, self.sum_done, self.step, self.var_done, self.rstd_done = sems(
            nc, stack, *(f"{tag}_{n}" for n in ("st_done", "sum_done", "mo_step", "var_done", "rstd_done")))

    def vector(self, dve):
        nc, (a, b, c, d) = self.nc, (self.work[:, n, :] for n in range(4))
        with dve.Fori(0, TILES) as i:
            nc.vector.bn_stats(self.stats[:, ds(i, 1), :].rearrange("p o f -> p (o f)"),
                               self.m.X[:, ds(i, 1), :].rearrange("p o d -> p (o d)")).then_inc(self.st_done, 1)
        dve.wait_ge(self.st_done, TILES)
        mean0, m20, mean1, m21 = (self.stats[:, :, n] for n in (1, 2, 4, 5))
        nc.vector.tensor_tensor(a, mean0, mean1, ALU.add).then_inc(self.sum_done, 1)
        nc.vector.tensor_tensor(b, mean0, mean1, ALU.subtract).then_inc(self.sum_done, 1)
        nc.vector.tensor_tensor(c, m20, m21, ALU.add).then_inc(self.sum_done, 1)
        dve.wait_ge(self.sum_done, 3)
        nc.vector.tensor_scalar(self.mean[:, :], a, 0.5, None, ALU.mult).then_inc(self.step, 1)
        nc.vector.scalar_tensor_tensor(out=d, in0=b, scalar=0.25, in1=b, op0=ALU.mult, op1=ALU.mult)\
            .then_inc(self.step, 1)
        dve.wait_ge(self.step, 2)
        nc.vector.scalar_tensor_tensor(out=a, in0=c, scalar=1.0 / D, in1=d, op0=ALU.mult, op1=ALU.add)\
            .then_inc(self.step, 1)
        dve.wait_ge(self.step, 3)
        nc.vector.tensor_scalar(self.var_eps[:, :], a, LN_EPS, None, ALU.add).then_inc(self.var_done, 1)
        dve.wait_ge(self.rstd_done, 1)

    def gpsimd(self, pool):
        pool.wait_ge(self.var_done, 1)
        self.nc.gpsimd.tensor_tensor(self.rstd[:, :], self.var_eps[:, :], self.m.neghalf[:, :], ALU.pow)\
            .then_inc(self.rstd_done, 1)

    def normalise(self, out, i):
        return self.nc.vector.tensor_scalar(out, self.m.X[:, ds(i, 1), :].rearrange("p o d -> p (o d)"),
                                            self.mean[:, ds(i, 1)], self.rstd[:, ds(i, 1)], ALU.subtract, ALU.mult)


def route(nc, m, tag, xs, io):
    with ExitStack() as st:
        def sb(name, shape, dt):
            return st.enter_context(nc.sbuf_tensor(f"{tag}_{name}", shape, dt))

        mo = Moments(nc, st, tag, m)
        ring = sb("ring", [P, 2, BT, D], F32)
        xt = sb("xt", [P, 2, KC, BLOCK], F32)
        wg = sb("wg", [P, KC, EXPERTS], F32)
        z = sb("z", [P, TILES, EXPERTS], F32)
        ez = sb("ez", [P, TILES, EXPERTS], F32)
        pick = sb("pick", [P, TILES, EXPERTS], F32)
        mask = sb("mask", [P, TILES, EXPERTS], BF16)
        loc8 = sb("loc8", [P, TILES, EXPERTS], F32)
        lmax, se, gate, cm, loc, keep, locc, base, slotf, drop = (
            sb(n, [P, TILES], F32) for n in
            ("lmax", "se", "gate", "cm", "loc", "keep", "locc", "base", "slotf", "drop"))
        xtp = [st.enter_context(nc.psum_tensor(f"{tag}_xtp{s}", [P, KC, BLOCK], F32)) for s in range(2)]
        lg = st.enter_context(nc.psum_tensor(f"{tag}_lg", [P, 512], F32))
        pos = st.enter_context(nc.psum_tensor(f"{tag}_pos", [P, 512], F32))
        (wg_loaded, xn_ready, xn_kept, xtp_ready, xt_ready, lg_ready,
         chain, z_ready, ez_ready, mask_ready, pos_ready, slot_ready, scattered) = sems(
            nc, st, *(f"{tag}_{n}" for n in (
                "wg_loaded", "xn_ready", "xn_kept", "xtp_ready",
                "xt_ready", "lg_ready", "chain", "z_ready", "ez_ready", "mask_ready", "pos_ready", "slot_ready",
                "scattered")))
        passed, = sems(nc, st, f"{tag}_passed")
        block = st.enter_context(nc.Block())

        @block.sync
        def _(sp):
            sp.dma_start(wg[:, :, :], io["wg"].rearrange("(c p) e -> p c e", p=P)).then_inc(wg_loaded, 16)

        @block.vector
        def _(dve):
            mo.vector(dve)
            def step(k, s):
                j = k * 2 + s
                wait_free(dve, xn_kept, k * 2)
                wait_free(dve, xtp_ready, k * 2)
                for t in range(BT):
                    i = j * BT + t
                    mo.normalise(ring[:, s, t, :], i).then_inc(xn_ready, 1)

            in_pairs(dve, BLOCKS, step)
            steps = [0]

            def link(ins):
                steps[0] += 1
                ins.then_inc(chain, 1)
                dve.wait_ge(chain, steps[0])

            def wide(a):
                return a[:, :].unsqueeze(2).to_broadcast([P, TILES, EXPERTS])

            dve.wait_ge(lg_ready, TILES)
            logits = lg[:, 0:TILES * EXPERTS].rearrange("p (i e) -> p i e", e=EXPERTS)
            link(nc.vector.tensor_reduce(lmax[:, :], logits, AX.X, ALU.max))
            nc.vector.tensor_tensor(z[:, :, :], logits, wide(lmax), ALU.subtract).then_inc(z_ready, 1)
            dve.wait_ge(z_ready, 1)
            link(nc.vector.tensor_scalar(pick[:, :, :], z[:, :, :], 0.0, None, ALU.is_ge))
            link(nc.vector.tensor_tensor(loc8[:, :, :], pick[:, :, :], m.rank[:, :, :], ALU.mult))
            link(nc.vector.tensor_reduce(cm[:, :], loc8[:, :, :], AX.X, ALU.max))
            nc.vector.tensor_tensor(mask[:, :, :], loc8[:, :, :], wide(cm), ALU.is_equal).then_inc(mask_ready, 1)
            dve.wait_ge(ez_ready, 1)
            link(nc.vector.tensor_reduce(se[:, :], ez[:, :, :], AX.X, ALU.add))
            link(nc.vector.reciprocal(gate[:, :], se[:, :]))
            link(nc.vector.tensor_scalar(base[:, :], cm[:, :], -float(CAP), float(CAP * EXPERTS), ALU.mult, ALU.add))
            dve.wait_ge(pos_ready, 1)
            dve.wait_ge(mask_ready, 1)
            link(nc.vector.tensor_tensor(pick[:, :, :], pos[:, 0:TILES * EXPERTS].rearrange("p (i e) -> p i e", e=EXPERTS),
                                         mask[:, :, :], ALU.mult))
            link(nc.vector.tensor_reduce(loc[:, :], pick[:, :, :], AX.X, ALU.add))
            link(nc.vector.tensor_scalar(keep[:, :], loc[:, :], float(CAP), None, ALU.is_lt))
            link(nc.vector.tensor_scalar(locc[:, :], loc[:, :], float(CAP - 1), None, ALU.min))
            link(nc.vector.scalar_tensor_tensor(out=m.hgate[:, :], in0=gate[:, :], scalar=0.5, in1=keep[:, :],
                                                op0=ALU.mult, op1=ALU.mult))
            link(nc.vector.tensor_tensor(slotf[:, :], base[:, :], locc[:, :], ALU.add))
            link(nc.vector.tensor_scalar(drop[:, :], keep[:, :], -2.0 * TOKENS, 2.0 * TOKENS, ALU.mult, ALU.add))
            nc.vector.tensor_copy(m.slot_get[:, :], slotf[:, :]).then_inc(slot_ready, 1)
            nc.vector.tensor_tensor(m.slot_put[:, :], slotf[:, :], drop[:, :], ALU.add).then_inc(slot_ready, 1)

        @block.gpsimd
        def _(pool):
            mo.gpsimd(pool)
            def step(k, s):
                j = k * 2 + s
                wait_alone(pool, xn_ready, j * BT + BT, passed)
                nc.gpsimd.tensor_copy(m.ROWS[:, ds(j * BT, BT), :], ring[:, s, :, :]).then_inc(xn_kept, 1)

            in_pairs(pool, BLOCKS, step)
            pool.wait_ge(xn_kept, BLOCKS)
            pool.wait_ge(slot_ready, 2)
            for i in range(TILES):
                nc.gpsimd.indirect_dma_start(
                    out=xs[:, :], out_offset=bass.IndirectOffsetOnAxis(ap=m.slot_put[:, i:i + 1], axis=0),
                    in_=m.ROWS[:, i, :], in_offset=None, bounds_check=TOKENS - 1,
                    oob_is_err=False).then_inc(scattered, 16)
            pool.wait_ge(scattered, 16 * TILES)

        @block.scalar
        def _(act):
            def step(k, s):
                j = k * 2 + s
                act.wait_ge(xtp_ready, j + 1)
                wait_free(act, lg_ready, k * 2 * BT)
                nc.scalar.activation(xt[:, s, :, :], xtp[s][:, :, :], ACT.Copy).then_inc(xt_ready, 1)

            in_pairs(act, BLOCKS, step)
            act.wait_ge(z_ready, 1)
            nc.scalar.activation(ez[:, :, :], z[:, :, :], ACT.Exp).then_inc(ez_ready, 1)

        @block.tensor
        def _(pe):
            pe.wait_ge(wg_loaded, 16)
            def step(k, s):
                j = k * 2 + s
                pe.wait_ge(xn_ready, j * BT + BT)
                for c in range(KC):
                    for t in range(BT):
                        last = pe.transpose(xtp[s][:, c, t * P:(t + 1) * P], ring[:, s, t, c * P:(c + 1) * P],
                                            m.ident_f[:, :])
                last.then_inc(xtp_ready, 1)
                pe.wait_ge(xt_ready, j + 1)
                for t in range(BT):
                    for c in range(KC):
                        last = pe.matmul(lg[:, ds((j * BT + t) * EXPERTS, EXPERTS)],
                                         xt[:, s, c, t * P:(t + 1) * P], wg[:, c, :],
                                         start=(c == 0), stop=(c == KC - 1))
                    last.then_inc(lg_ready, 1)

            in_pairs(pe, BLOCKS, step)
            pe.wait_ge(mask_ready, 1)
            flat = mask[:, :, :].rearrange("p i e -> p (i e)")
            pe.matmul(pos[:, 0:TILES * EXPERTS], m.before[:, :], flat, start=True, stop=False)
            for i in range(TILES - 1):
                later = TILES - 1 - i
                last = pe.matmul(pos[:, (i + 1) * EXPERTS:TILES * EXPERTS].rearrange("p (i e) -> p i e", e=EXPERTS),
                                 m.ones_b[:, :], mask[:, i:i + 1, :].to_broadcast([P, later, EXPERTS]),
                                 start=False, stop=(i == TILES - 2))
            last.then_inc(pos_ready, 1)


def experts(nc, m, tag, xs, ys, io):
    with ExitStack() as st:
        def sb(name, shape, dt):
            return st.enter_context(nc.sbuf_tensor(f"{tag}_{name}", shape, dt))

        weights = sb("we", [P, EXPERTS, KC, D], F32)
        bias = sb("be", [P, EXPERTS, D], F32)
        xe = sb("xe", [P, 2, BT, D], F32)
        xt = sb("xet", [P, 2, KC, BLOCK], F32)
        ye = sb("ye", [P, 2, BT, D], F32)
        xtp = st.enter_context(nc.psum_tensor(f"{tag}_xetp", [P, 2, KC, BLOCK], F32))
        yp = st.enter_context(nc.psum_tensor(f"{tag}_yp", [P, 2, BT, D], F32))
        w_loaded, xe_loaded0, xe_loaded1, xtp_ready, xt_ready, yp_ready, ye_ready, stored0, stored1 = sems(
            nc, st, *(f"{tag}_{n}" for n in ("w_loaded", "xe_loaded0", "xe_loaded1", "xetp_ready", "xet_ready",
                                             "yp_ready", "ye_ready", "ye_stored0", "ye_stored1")))
        xe_loaded, stored = (xe_loaded0, xe_loaded1), (stored0, stored1)
        block = st.enter_context(nc.Block())

        @block.sync
        def _(sp):
            def step(k, s):
                e = k * 2 + s
                wait_free(sp, xtp_ready, k * 2)
                sp.dma_start(xe[:, s, :, :], xs[ds(e * CAP, CAP), :].rearrange("(t p) d -> p t d", p=P))\
                    .then_inc(xe_loaded[s], 16)

            in_pairs(sp, EXPERTS, step)

        @block.scalar
        def _(act):
            act.dma_start(weights[:, :, :, :], io["w_t"].rearrange("e (c p) f -> p e c f", p=P)).then_inc(w_loaded, 16)
            act.dma_start(bias[:, :, :], io["b"].unsqueeze(0).to_broadcast([P, EXPERTS, D])).then_inc(w_loaded, 16)
            def step(k, s):
                act.wait_ge(xtp_ready, k * 2 + s + 1)
                wait_free(act, yp_ready, k * 2)
                nc.scalar.activation(xt[:, s, :, :], xtp[:, s, :, :], ACT.Copy).then_inc(xt_ready, 1)

            in_pairs(act, EXPERTS, step)

        @block.tensor
        def _(pe):
            pe.wait_ge(w_loaded, 32)
            def step(k, s):
                e = k * 2 + s
                pe.wait_ge(xe_loaded[s], k * 16 + 16)
                wait_free(pe, xt_ready, k * 2)
                for c in range(KC):
                    for t in range(BT):
                        last = pe.transpose(xtp[:, s, c, t * P:(t + 1) * P], xe[:, s, t, c * P:(c + 1) * P],
                                            m.ident_f[:, :])
                last.then_inc(xtp_ready, 1)
                pe.wait_ge(xt_ready, e + 1)
                wait_free(pe, ye_ready, k * 2)
                for t in range(BT):
                    for c in range(KC):
                        last = pe.matmul(yp[:, s, t, :], xt[:, s, c, t * P:(t + 1) * P],
                                         weights[:, ds(e, 1), c, :],
                                         start=(c == 0), stop=(c == KC - 1))
                last.then_inc(yp_ready, 1)

            in_pairs(pe, EXPERTS, step)

        @block.vector
        def _(dve):
            dve.wait_ge(w_loaded, 32)
            def step(k, s):
                e = k * 2 + s
                dve.wait_ge(yp_ready, e + 1)
                wait_free(dve, stored[s], k * 16)
                nc.vector.tensor_tensor(ye[:, s, :, :], yp[:, s, :, :],
                                        bias[:, ds(e, 1), :].to_broadcast([P, BT, D]), ALU.add)\
                    .then_inc(ye_ready, 1)

            in_pairs(dve, EXPERTS, step)

        @block.gpsimd
        def _(pool):
            def step(k, s):
                e = k * 2 + s
                pool.wait_ge(ye_ready, e + 1)
                pool.dma_start(ys[ds(e * CAP, CAP), :].rearrange("(t p) d -> p t d", p=P), ye[:, s, :, :])\
                    .then_inc(stored[s], 16)

            in_pairs(pool, EXPERTS, step)
            for s in range(2):
                pool.wait_ge(stored[s], EXPERTS // 2 * 16)


def combine(nc, m, tag, ys, io, last_layer):
    CG = 8
    with ExitStack() as st:
        gathered = sems(nc, st, *(f"{tag}_gathered{g}" for g in range(TILES // CG)))
        x_ready, out_stored = sems(nc, st, f"{tag}_x_ready", f"{tag}_out_stored")
        block = st.enter_context(nc.Block())

        @block.gpsimd
        def _(pool):
            for i in range(TILES):
                nc.gpsimd.indirect_dma_start(
                    out=m.ROWS[:, i, :], out_offset=None, in_=ys[:, :],
                    in_offset=bass.IndirectOffsetOnAxis(ap=m.slot_get[:, i:i + 1], axis=0)).then_inc(gathered[i // CG], 16)

        @block.vector
        def _(dve):
            for g in range(TILES // CG):
                dve.wait_ge(gathered[g], 16 * CG)
                with dve.Fori(g * CG, (g + 1) * CG) as i:
                    nc.vector.scalar_tensor_tensor(
                        out=m.X[:, ds(i, 1), :].rearrange("p o d -> p (o d)"),
                        in0=m.ROWS[:, ds(i, 1), :].rearrange("p o d -> p (o d)"), scalar=m.hgate[:, ds(i, 1)],
                        in1=m.X[:, ds(i, 1), :].rearrange("p o d -> p (o d)"),
                        op0=ALU.mult, op1=ALU.add).then_inc(x_ready, 1)

        if last_layer:
            @block.sync
            def _(sp):
                for g in range(TILES // CG):
                    sp.wait_ge(x_ready, (g + 1) * CG)
                    sp.dma_start(io["out"][g * CG * P:(g + 1) * CG * P, :].rearrange("(i p) d -> p i d", p=P),
                                 m.X[:, g * CG:(g + 1) * CG, :]).then_inc(out_stored, 16)
                sp.wait_ge(out_stored, 16 * (TILES // CG))


def project(nc, m, io):
    with ExitStack() as st:
        def sb(name, shape, dt):
            return st.enter_context(nc.sbuf_tensor(f"pr_{name}", shape, dt))

        mo = Moments(nc, st, "pr", m)
        ring = sb("ring", [P, 2, BT, D], F32)
        xt = sb("xt", [P, 2, KC, BLOCK], F32)
        w = sb("w", [P, 3, KC, D], F32)
        parts = sb("parts", [P, 2, 2, PARTS, KC, BLOCK], BF16)
        rest = sb("rest", [P, 2, 2, KC * BLOCK], F32)
        vals = sb("vals", [P, 2, BT, D], F32)
        xtp = st.enter_context(nc.psum_tensor("pr_xtp", [P, KC, BLOCK], F32))
        qkp = [st.enter_context(nc.psum_tensor(f"pr_{n}p", [P, KC, BLOCK], F32)) for n in "qk"]
        vp = st.enter_context(nc.psum_tensor("pr_vp", [P, BT, D], F32))
        (w_loaded, xn_ready, xtp_ready, xt_ready, v_ready, v_out,
         stored0, stored1) = sems(
            nc, st, *(f"pr_{n}" for n in ("w_loaded", "xn_ready",
                                          "xtp_ready", "xt_ready", "v_ready", "v_out", "stored0", "stored1")))
        qk_ready = sems(nc, st, "pr_q_ready", "pr_k_ready")
        part1 = sems(nc, st, "pr_q_part1", "pr_k_part1")
        rest1 = sems(nc, st, "pr_q_rest", "pr_k_rest")
        part2 = sems(nc, st, "pr_q_part2", "pr_k_part2")
        part3 = sems(nc, st, "pr_q_part3", "pr_k_part3")
        stored = (stored0, stored1)
        dmas = 2 * PARTS + BT
        scale = (SCALE, 1.0)
        passed, = sems(nc, st, "project_passed")
        block = st.enter_context(nc.Block())
        half = BLOCKS // BATCH // 2

        @block.vector
        def _(dve):
            mo.vector(dve)
            def step(k, s):
                j = k * 2 + s
                wait_free(dve, xtp_ready, k * 2)
                for t in range(BT):
                    i = j * BT + t
                    mo.normalise(ring[:, s, t, :], i).then_inc(xn_ready, 1)
                for n in range(2):
                    dve.wait_ge(qk_ready[n], j + 1)
                    dve.wait_ge(part1[n], j + 1)
                    wait_free(dve, part3[n], k * 2)
                    nc.vector.scalar_tensor_tensor(
                        out=rest[:, s, n, :], in0=qkp[n][:, :, :].rearrange("p c t -> p (c t)"), scalar=scale[n],
                        in1=parts[:, s, n, 0, :, :].rearrange("p c t -> p (c t)"), op0=ALU.mult,
                        op1=ALU.subtract).then_inc(rest1[n], 1)

            in_pairs(dve, BLOCKS, step)

        @block.gpsimd
        def _(pool):
            mo.gpsimd(pool)
            def step(k, s):
                j = k * 2 + s
                wait_free(pool, stored[s], k * dmas * 16)
                for n in range(2):
                    wait_alone(pool, rest1[n], j + 1, passed)
                    nc.gpsimd.tensor_copy(parts[:, s, n, 1, :, :].rearrange("p c t -> p (c t)"), rest[:, s, n, :])\
                        .then_inc(part2[n], 1)
                    pool.wait_ge(part2[n], j + 1)
                    nc.gpsimd.tensor_tensor(parts[:, s, n, 2, :, :].rearrange("p c t -> p (c t)"), rest[:, s, n, :],
                                            parts[:, s, n, 1, :, :].rearrange("p c t -> p (c t)"), ALU.subtract)\
                        .then_inc(part3[n], 1)

            in_pairs(pool, BLOCKS, step)

        @block.scalar
        def _(act):
            def step(k, s):
                j = k * 2 + s
                act.wait_ge(xtp_ready, j + 1)
                wait_free(act, v_ready, k * 2)
                nc.scalar.activation(xt[:, s, :, :], xtp[:, :, :], ACT.Copy).then_inc(xt_ready, 1)
                wait_free(act, stored[s], k * dmas * 16)
                for n in range(2):
                    act.wait_ge(qk_ready[n], j + 1)
                    nc.scalar.activation(parts[:, s, n, 0, :, :], qkp[n][:, :, :], ACT.Copy, scale=scale[n])\
                        .then_inc(part1[n], 1)
                act.wait_ge(v_ready, j + 1)
                nc.scalar.activation(vals[:, s, :, :], vp[:, :, :], ACT.Copy).then_inc(v_out, 1)

            in_pairs(act, BLOCKS, step)

        @block.tensor
        def _(pe):
            pe.wait_ge(w_loaded, 16 * 3)
            def step(k, s):
                j = k * 2 + s
                pe.wait_ge(xn_ready, j * BT + BT)
                wait_free(pe, xt_ready, j)
                for c in range(KC):
                    for t in range(BT):
                        last = pe.transpose(xtp[:, c, t * P:(t + 1) * P], ring[:, s, t, c * P:(c + 1) * P],
                                            m.ident_f[:, :])
                last.then_inc(xtp_ready, 1)
                pe.wait_ge(xt_ready, j + 1)
                for n in range(2):
                    wait_free(pe, rest1[n], j)
                    for co in range(KC):
                        for c in range(KC):
                            last = pe.matmul(qkp[n][:, co, :], w[:, n, c, co * P:(co + 1) * P], xt[:, s, c, :],
                                             start=(c == 0), stop=(c == KC - 1))
                    last.then_inc(qk_ready[n], 1)
                wait_free(pe, v_out, j)
                for t in range(BT):
                    for c in range(KC):
                        last = pe.matmul(vp[:, t, :], xt[:, s, c, t * P:(t + 1) * P], w[:, 2, c, :],
                                         start=(c == 0), stop=(c == KC - 1))
                last.then_inc(v_ready, 1)

            in_pairs(pe, BLOCKS, step)

        @block.sync
        def _(sp):
            for n, name in enumerate(("wq_t", "wk_t", "wv_t")):
                sp.dma_start(w[:, n, :, :], io[name].rearrange("(c p) f -> p c f", p=P)).then_inc(w_loaded, 16)
            with sp.Fori(0, BATCH) as b:
                with sp.Fori(0, half) as k:
                    for s in range(2):
                        j = b * (2 * half) + k * 2 + s
                        tok = k * (2 * BLOCK) + s * BLOCK
                        for n in range(2):
                            sp.wait_ge(part3[n], j + 1)
                            for part in range(PARTS):
                                sp.dma_start(m.QK[n][ds(b, 1), part, :, ds(tok, BLOCK)]
                                             .rearrange("o (c p) t -> p (o c) t", p=P),
                                             parts[:, s, n, part, :, :]).then_inc(stored[s], 16)
                        sp.wait_ge(v_out, j + 1)
                        for t in range(BT):
                            sp.dma_start(m.V[ds(b * GH, GH), ds(tok + t * P, P), :].rearrange("g p f -> p g f"),
                                         vals[:, s, t, :].rearrange("p (g f) -> p g f", f=GF)).then_inc(stored[s], 16)
            for s in range(2):
                sp.wait_ge(stored[s], BLOCKS // 2 * dmas * 16)


def attend(nc, m):
    with ExitStack() as st:
        def sb(name, shape, dt):
            return st.enter_context(nc.sbuf_tensor(f"at_{name}", shape, dt))

        def ps(name, shape, dt=F32):
            return st.enter_context(nc.psum_tensor(f"at_{name}", shape, dt))

        Q = [sb(f"q{s}", [AROWS, GH, SEQ], BF16) for s in range(2)]
        K = [sb(f"k{s}", [AROWS, GH, SEQ], BF16) for s in range(2)]
        V = [sb(f"v{s}", [P, QT * GH, 2 * DH], F32) for s in range(2)]
        v_raw = sb("vr", [P, QT * GH, DH], F32)
        ex = [sb(f"e{r}", [P, GH, WIN], F32) for r in range(ERING)]
        part_max = [sb(f"pm{s}", [P, GH, QT, WINS], F32) for s in range(2)]
        neg_max = sb("nm", [P, GH * QT], F32)
        left = sb("left", [P, 2, GH * QT], F32)
        max_parts = sb("mp", [P, PARTS, GH * QT], BF16)
        max_rows = sb("mr", [GH * EARLY_T, PARTS, P], BF16)
        junk = sb("junk", [P, 2, WIN], BF16)
        osb = sb("osb", [P, WIN], F32)
        den = sb("den", [P, 2, BT * GH], F32)
        score = [ps(f"s{h}", [P, 2, WIN]) for h in range(2)]
        chunk_ps = [ps(f"m{h}", [P, WIN]) for h in range(2)]
        sums = ps("o", [P, WIN])
        aux = ps("aux", [P, WIN])

        (scores_ready, exp_done, pv_done, masked, chunk_ready, chunk_read, max_step, max_split, aux_ready, aux_free,
         rows_ready, rows_stored, rows_early, rows_late, o_out, norm_step, filled) = sems(
            nc, st, *(f"at_{n}" for n in (
                "scores_ready", "exp_done", "pv_done", "masked", "chunk_ready", "chunk_read", "max_step", "max_split",
                "aux_ready", "aux_free", "rows_ready", "rows_stored", "rows_early", "rows_late", "o_out", "norm_step",
                "filled")))
        quarter = [[sems(nc, st, f"at_in{s}_{w}")[0] for w in range(WINS)] for s in range(2)]
        v_in, v_laid = sems(nc, st, "at_v_in", "at_v_laid")
        passed, = sems(nc, st, "attend_passed")
        block = st.enter_context(nc.Block())

        QROWS = [(0, 0), (1, 0), (2, 0), (3, 1), (4, 1), (5, 2)]
        KROWS = [(0, 0), (1, 1), (2, 2), (3, 0), (4, 1), (5, 0)]
        qdmas = len(QROWS) + len(KROWS)
        DIAG = sum(1 for w, kb in UNITS if kb * P >= w * WIN)

        def raised(g, per, plus=0):
            return g * per + (plus + 1)

        def per_group(g, per, plus=0):
            return g * per + plus

        def groups(eng, body, first=0):
            with eng.Fori(0, GROUPS // 2 - 1) as i:
                for s in range(2):
                    body(i * 2 + s, s, True)
            body(GROUPS - 2, 0, True)
            body(GROUPS - 1, 1, False)

        UNIT_OF_LATE, UNIT_OF_EARLY, FLUSH = 5, 28, 3
        after = [0] * NU
        for k in range(NC_):
            after[1 + k * (NU - 2) // NC_] += 1
        assert sum(after) == NC_
        assert sum(after[:UNIT_OF_EARLY]) >= EARLY_CHUNKS
        first_chunk = [sum(after[:n]) for n in range(NU)]

        first_unit = [n for n, (w, kb) in enumerate(UNITS) if kb == 0]
        order = sorted([(UNIT_OF_LATE, "late"), (UNIT_OF_EARLY, "early")]
                       + [(first_unit[w + 1] + FLUSH, w) for w in range(WINS - 1)] + [(NU, WINS - 1)], key=lambda a: a[0])
        assert len(order) == AUX_USES

        def uses(what, nxt=True):
            names = [x for _, x in order if nxt or x != "early"]
            return names.index(what) + 1

        def use_before(what, nxt=True):
            names = [None] + [x for _, x in order if nxt or x != "early"]
            return names[names.index(what) - 1]

        @block.sync
        def _(sp):
            def load(gb, hg, s, earlier):
                for w in range(WINS):
                    for buf, dram, rows in ((Q[s], m.QK[0], QROWS), (K[s], m.QK[1], KROWS)):
                        for r, part in rows:
                            sp.dma_start(buf[r * DH:(r + 1) * DH, :, w * WIN:(w + 1) * WIN],
                                         dram[ds(gb, 1), part, ds(hg * GF, GF), w * WIN:(w + 1) * WIN]
                                         .rearrange("o (h d) t -> d (o h) t", d=DH)).then_inc(quarter[s][w], 16)
                if earlier is not None:
                    sp.wait_ge(v_laid, earlier)
                sp.dma_start(v_raw[:, :, :].rearrange("p (k h) d -> p k (h d)", h=GH),
                             m.V[ds(gb * GH + hg, 1), :, :].rearrange("o (k p) f -> p (o k) f", p=P)).then_inc(v_in, 16)

            def max_rows_in(g, s, early):
                t0, nt = (0, EARLY_T) if early else (EARLY_T, QT - EARLY_T)
                dram = m.MAXROWS[0 if early else 1]
                done = per_group(g, 2, 1 if early else 2)
                wait_alone(sp, rows_early if early else rows_late, per_group(g, 16), passed)
                wait_alone(sp, rows_ready, done, passed)
                sp.dma_start(dram.rearrange("c r x -> r c x"), max_rows[0:GH * nt, :, :]).then_inc(rows_stored, 16)
                sp.wait_ge(rows_stored, done * 16)
                sp.dma_start(Q[s][ROWS:AROWS, :, t0 * P:(t0 + nt) * P],
                             dram.rearrange("c (h t) x -> c h (t x)", h=GH)).then_inc(rows_early if early else rows_late, 16)

            def step(g, s, nxt, nb=None, nh=None):
                max_rows_in(g, s, False)
                if nxt:
                    max_rows_in(g + 1, 1 - s, True)
                if nb is not None:
                    sp.wait_ge(pv_done, raised(g, NU, NU))
                    load(nb, nh, s, g + 2)

            load(0, 0, 0, None)
            load(0, 1, 1, 1)
            max_rows_in(0, 0, True)
            step(0, 0, True, 0, 2)
            step(1, 1, True, 0, 3)
            with sp.Fori(1, GROUPS // 2 - 1) as i:
                for s in range(2):
                    step(i * 2 + s, s, True, 1, i * 2 - 2 + s)
            step(GROUPS - 2, 0, True)
            step(GROUPS - 1, 1, False)

        @block.gpsimd
        def _(pool):
            def lay_values(g, s):
                pool.wait_ge(filled, 6)
                wait_alone(pool, v_in, per_group(g, 16, 16), passed)
                nc.gpsimd.tensor_copy(V[s][:, :, 0:DH], v_raw[:, :, :]).then_inc(v_laid, 1)

            def step(g, s, nxt):
                for n, (w, kb) in enumerate(UNITS):
                    off = kb * P - w * WIN
                    if nxt and n == NU // 2:
                        lay_values(g + 1, 1 - s)
                    if off < 0:
                        continue
                    wait_alone(pool, exp_done, raised(g, 2 * NU, 2 * n + 2), passed)
                    tri = ex[n % ERING][:, :, off:off + P]
                    nc.gpsimd.affine_select(out=tri, in_=tri, compare_op=ALU.is_ge, fill=0.0, base=0,
                                            pattern=[[0, GH], [1, P]], channel_multiplier=-1).then_inc(masked, 1)

            lay_values(0, 0)
            groups(pool, step)

        @block.scalar
        def _(act):
            def rows_out(g, early, uses):
                nt = EARLY_T if early else QT - EARLY_T
                act.wait_ge(aux_ready, uses)
                act.wait_ge(rows_stored, per_group(g, 32, 0 if early else 16))
                nc.scalar.activation(max_rows[0:GH * nt, :, :],
                                     aux[0:GH * nt, 0:PARTS * P // 2].bitcast(BF16).rearrange("r (c x) -> r c x", c=PARTS),
                                     ACT.Copy).then_inc(rows_ready, 1)

            def window_out(g, w, unit):
                act.wait_ge(pv_done, raised(g, NU, unit))
                act.wait_ge(aux_ready, per_group(g, AUX_USES, 1 + (uses(w - 1) if w else 0)))
                nc.scalar.activation(osb[:, :], sums[:, :], ACT.Copy).then_inc(o_out, 1)

            def step(g, s, nxt):
                for n, (w, kb) in enumerate(UNITS):
                    off = max(0, kb * P - w * WIN)
                    if n < ERING:
                        act.wait_ge(pv_done, raised(g, NU))
                    else:
                        act.wait_ge(pv_done, raised(g, NU, n - ERING + 1))
                    for half in range(2):
                        act.wait_ge(scores_ready, per_group(g, 2 * NU, 2 * n + half + 1))
                        nc.scalar.activation(ex[n % ERING][:, 2 * half:2 * half + 2, off:WIN],
                                             score[half][:, :, off:WIN], ACT.Exp).then_inc(exp_done, 1)
                    if w > 0 and kb == 0:
                        window_out(g, w - 1, n)
                    if n == UNIT_OF_LATE + 1:
                        rows_out(g, False, per_group(g, AUX_USES, 1 + uses("late")))
                    if nxt and n == UNIT_OF_EARLY + 1:
                        rows_out(g + 1, True, per_group(g, AUX_USES, 1 + uses("early")))
                window_out(g, WINS - 1, NU)

            act.sem_inc(pv_done, 1)
            act.wait_ge(aux_ready, 1)
            nc.scalar.activation(max_rows[0:GH * EARLY_T, :, :],
                                 aux[0:GH * EARLY_T, 0:PARTS * P // 2].bitcast(BF16)
                                 .rearrange("r (c x) -> r c x", c=PARTS), ACT.Copy).then_inc(rows_ready, 1)
            groups(act, step)

        @block.vector
        def _(dve):
            def chunk(g, s, k):
                t, h, c, width = CHUNKS[k]
                out = part_max[s][:, h, t, c:c + 1]
                if c == t // BT:
                    if k >= 2:
                        dve.wait_ge(chunk_read, per_group(g, NC_, k - 1))
                    wait_alone(dve, chunk_ready, per_group(g, NC_, k + 1), passed)
                    nc.vector.tensor_tensor_reduce(
                        out=junk[:, k % 2, 0:width], in0=chunk_ps[k % 2][:, 0:width],
                        in1=m.maskneg[:, WIN - width:WIN], scale=1.0, scalar=NEG,
                        op0=ALU.add, op1=ALU.max, accum_out=out).then_inc(chunk_read, 1)
                else:
                    dve.wait_ge(chunk_ready, per_group(g, NC_, k + 1))
                    nc.vector.tensor_reduce(out, chunk_ps[k % 2][:, 0:width], AX.X, ALU.max).then_inc(chunk_read, 1)

            def split(g, s, early):
                t0, nt = (0, EARLY_T) if early else (EARLY_T, QT - EARLY_T)
                n = GH * nt
                done = [0]
                start = per_group(g, 2 * 5, 0 if early else 5)

                def link(ins):
                    done[0] += 1
                    ins.then_inc(max_step, 1)
                    dve.wait_ge(max_step, start + done[0])

                dve.wait_ge(chunk_read, per_group(g, NC_, EARLY_CHUNKS if early else NC_))
                link(nc.vector.tensor_reduce(neg_max[:, 0:n].rearrange("p (h t) -> p h t", h=GH),
                                             part_max[s][:, :, t0:t0 + nt, :], AX.X, ALU.max, negate=True))
                dve.wait_ge(aux_ready, AUX_BEFORE(g, early))
                link(nc.vector.tensor_copy(max_parts[:, 0, 0:n], neg_max[:, 0:n]))
                link(nc.vector.tensor_tensor(left[:, 0, 0:n], neg_max[:, 0:n], max_parts[:, 0, 0:n], ALU.subtract))
                link(nc.vector.tensor_copy(max_parts[:, 1, 0:n], left[:, 0, 0:n]))
                link(nc.vector.tensor_tensor(max_parts[:, 2, 0:n], left[:, 0, 0:n], max_parts[:, 1, 0:n], ALU.subtract))

            def AUX_BEFORE(g, early):
                if early:
                    return 0 if isinstance(g, int) and g == 0 else per_group(g - 1, AUX_USES, 1 + uses("late"))
                return per_group(g, AUX_USES, 1)

            def normalise(g, w, nxt=True):
                dve.wait_ge(aux_ready, per_group(g, AUX_USES, 1 + uses(w, nxt)))
                start = per_group(g, 2 * WINS, 2 * w)
                view = aux[:, :].rearrange("p (t h a f) -> p (t h) a f", t=BT, h=GH, a=2)
                nc.vector.tensor_scalar(den[:, 0, :], view[:, :, 1, 0:1].rearrange("p n f -> p (n f)"), DEN_EPS, None,
                                        ALU.add).then_inc(norm_step, 1)
                dve.wait_ge(norm_step, start + 1)
                nc.vector.reciprocal(den[:, 1, :], den[:, 0, :]).then_inc(norm_step, 1)
                dve.wait_ge(norm_step, start + 2)
                nc.vector.tensor_tensor(
                    m.AT[:, ds(g * QT + w * BT, BT), :].rearrange("p t (h d) -> p (t h) d", h=GH), view[:, :, 0, :],
                    den[:, 1, :].unsqueeze(2).to_broadcast([P, BT * GH, DH]), ALU.mult).then_inc(aux_free, 1)
                dve.wait_ge(aux_free, raised(g, WINS, w + 1))

            def step(g, s, nxt):
                for n in range(NU):
                    if nxt:
                        for k in range(first_chunk[n], first_chunk[n] + after[n]):
                            chunk(g + 1, 1 - s, k)
                    if n == UNIT_OF_LATE - 2:
                        split(g, s, False)
                    if nxt and n == UNIT_OF_EARLY - 1:
                        split(g + 1, 1 - s, True)
                    for w in range(WINS - 1):
                        if n == first_unit[w + 1] + FLUSH:
                            normalise(g, w)
                normalise(g, WINS - 1, nxt)

            for s in range(2):
                nc.vector.memset(K[s][ROWS:AROWS, :, :], 1.0).then_inc(filled, 1)
                nc.vector.memset(V[s][:, :, DH:2 * DH], 1.0).then_inc(filled, 1)
                nc.vector.memset(part_max[s][:, :, :, :], NEG).then_inc(filled, 1)
            dve.wait_ge(filled, 6)
            for k in range(NC_):
                chunk(0, 0, k)
                if k == EARLY_CHUNKS - 1:
                    split(0, 0, True)
            groups(dve, step)

        @block.tensor
        def _(pe):
            def chunk(g, s, k, visit):
                t, h, c, width = CHUNKS[k]
                if k == 0 or CHUNKS[k - 1][0] // BT != t // BT:
                    pe.wait_ge(quarter[s][t // BT], visit * 16 * qdmas)
                pe.wait_ge(chunk_read, per_group(g, NC_, k - 1) if k >= 2 else per_group(g, NC_))
                pe.matmul(chunk_ps[k % 2][:, 0:width], Q[s][0:ROWS, h, t * P:(t + 1) * P],
                          K[s][0:ROWS, h, c * WIN:c * WIN + width], start=True, stop=True).then_inc(chunk_ready, 1)

            def rows(g, early, split_count):
                nt = EARLY_T if early else QT - EARLY_T
                n = GH * nt
                wait_alone(pe, max_step, split_count, passed)
                for c in range(PARTS):
                    last = pe.transpose(aux[0:n, c * P // 2:(c + 1) * P // 2].bitcast(BF16), max_parts[:, c, 0:n],
                                        m.ident_b[:, :])
                last.then_inc(aux_ready, 1)

            def window(g, w):
                pe.wait_ge(o_out, raised(g, WINS, w + 1))
                for t in range(BT):
                    last = pe.transpose(aux[:, t * P:(t + 1) * P], osb[:, t * P:(t + 1) * P], m.ident_f[:, :])
                last.then_inc(aux_ready, 1)

            def aux_wait(g, what, nxt=True):
                prev = use_before(what, nxt)
                if prev is None:
                    pe.wait_ge(aux_free, raised(g, WINS))
                    pe.wait_ge(rows_ready, per_group(g, 2, 1))
                elif prev == "late":
                    pe.wait_ge(rows_ready, per_group(g, 2, 2))
                elif prev == "early":
                    pe.wait_ge(rows_ready, per_group(g, 2, 3))
                else:
                    pe.wait_ge(aux_free, raised(g, WINS, prev + 1))

            def pv(g, s, n):
                w, kb = UNITS[n]
                off = max(0, kb * P - w * WIN)
                if kb * P >= w * WIN:
                    diag = sum(1 for ww, kk in UNITS[:n + 1] if kk * P >= ww * WIN)
                    pe.wait_ge(masked, per_group(g, DIAG, diag))
                else:
                    pe.wait_ge(exp_done, raised(g, 2 * NU, 2 * n + 2))
                if kb == 0:
                    pe.wait_ge(o_out, raised(g, WINS, w))
                for h in range(GH):
                    last = pe.matmul(sums[32 * h:32 * h + 32, off:WIN], V[s][:, kb * GH + h, :], ex[n % ERING][:, h, off:WIN],
                                     start=(kb == 0), stop=(kb == (w + 1) * WIN // P - 1))
                last.then_inc(pv_done, 1)
                return last

            def step(g, s, nxt):
                pe.wait_ge(rows_early, per_group(g, 16, 16))
                for n, (w, kb) in enumerate(UNITS):
                    off = max(0, kb * P - w * WIN)
                    if n == first_unit[EARLY_T // BT]:
                        pe.wait_ge(rows_late, per_group(g, 16, 16))
                    todo = list(range(first_chunk[n], first_chunk[n] + after[n])) if nxt else []
                    for half in range(2):
                        pe.wait_ge(exp_done, raised(g, 2 * NU, 2 * n - 1 + half if n else 0))
                        for h in range(2):
                            hh = 2 * half + h
                            last = pe.matmul(score[half][:, h, off:WIN], K[s][:, hh, kb * P:(kb + 1) * P],
                                             Q[s][:, hh, w * WIN + off:(w + 1) * WIN], start=True, stop=True)
                        last.then_inc(scores_ready, 1)
                        if todo:
                            chunk(g + 1, 1 - s, todo.pop(0), next_visit(g, s))
                    if n == 0:
                        pe.wait_ge(v_laid, g + 1)
                    if n:
                        pv(g, s, n - 1)
                    while todo:
                        chunk(g + 1, 1 - s, todo.pop(0), next_visit(g, s))
                    if n == UNIT_OF_LATE:
                        aux_wait(g, "late")
                        rows(g, False, per_group(g, 10, 10))
                    if nxt and n == UNIT_OF_EARLY:
                        aux_wait(g, "early")
                        rows(g + 1, True, per_group(g, 10, 15))
                    for ww in range(WINS - 1):
                        if n == first_unit[ww + 1] + FLUSH:
                            aux_wait(g, ww)
                            window(g, ww)
                pv(g, s, NU - 1)
                aux_wait(g, WINS - 1, nxt)
                window(g, WINS - 1)

            def next_visit(g, s):
                return VISIT[0] + 1 + s

            VISIT = [0]
            pe.wait_ge(filled, 6)
            for sem in (exp_done, aux_free, o_out):
                pe.sem_inc(sem, 1)
            for k in range(NC_):
                chunk(0, 0, k, 1)
                if k == EARLY_CHUNKS + 2:
                    rows(0, True, 5)
            with pe.Fori(0, GROUPS // 2 - 1) as i:
                VISIT[0] = i
                for s in range(2):
                    step(i * 2 + s, s, True)
            VISIT[0] = GROUPS // 2 - 1
            step(GROUPS - 2, 0, True)
            step(GROUPS - 1, 1, False)


def output(nc, m, io):
    with ExitStack() as st:
        def sb(name, shape, dt):
            return st.enter_context(nc.sbuf_tensor(f"op_{name}", shape, dt))

        rows = sb("rows", [P, 2, BT, D], F32)
        at = sb("at", [P, 2, KC, BLOCK], F32)
        wo = sb("wo", [P, KC, D], F32)
        atp = st.enter_context(nc.psum_tensor("op_atp", [P, 2, KC, BLOCK], F32))
        yp = st.enter_context(nc.psum_tensor("op_yp", [P, 2, BT, D], F32))
        w_loaded, rows_ready, atp_ready, at_ready, y_ready, x_ready = sems(
            nc, st, *(f"op_{n}" for n in ("w_loaded", "rows_ready", "atp_ready", "at_ready", "y_ready", "x_ready")))
        half = BLOCKS // BATCH // 2
        passed, = sems(nc, st, "output_passed")
        block = st.enter_context(nc.Block())

        @block.sync
        def _(sp):
            sp.dma_start(wo[:, :, :], io["wo_t"].rearrange("(c p) f -> p c f", p=P)).then_inc(w_loaded, 16)

        @block.gpsimd
        def _(pool):
            def step(b, k, s):
                if b or not isinstance(k, int) or k:
                    wait_alone(pool, atp_ready, k * 2 + b * (2 * half), passed)
                for hg in range(HEADS // GH):
                    nc.gpsimd.tensor_copy(rows[:, s, :, hg * GF:(hg + 1) * GF],
                                          m.AT[:, ds(k * (2 * BT) + (b * GH + hg) * QT + s * BT, BT), :])\
                        .then_inc(rows_ready, 1)

            for b in range(BATCH):
                if b == 0:
                    for s in range(2):
                        step(0, 0, s)
                with pool.Fori(1 - b, half) as k:
                    for s in range(2):
                        step(b, k, s)

        @block.scalar
        def _(act):
            def step(k, s):
                act.wait_ge(atp_ready, k * 2 + s + 1)
                wait_free(act, y_ready, k * 2)
                nc.scalar.activation(at[:, s, :, :], atp[:, s, :, :], ACT.Copy).then_inc(at_ready, 1)

            in_pairs(act, BLOCKS, step)

        @block.tensor
        def _(pe):
            pe.wait_ge(w_loaded, 16)
            def step(k, s):
                j = k * 2 + s
                pe.wait_ge(rows_ready, j * (HEADS // GH) + HEADS // GH)
                wait_free(pe, at_ready, k * 2)
                for c in range(KC):
                    for t in range(BT):
                        last = pe.transpose(atp[:, s, c, t * P:(t + 1) * P], rows[:, s, t, c * P:(c + 1) * P],
                                            m.ident_f[:, :])
                last.then_inc(atp_ready, 1)
                pe.wait_ge(at_ready, j + 1)
                wait_free(pe, x_ready, k * 2)
                for t in range(BT):
                    for c in range(KC):
                        last = pe.matmul(yp[:, s, t, :], at[:, s, c, t * P:(t + 1) * P], wo[:, c, :],
                                         start=(c == 0), stop=(c == KC - 1))
                last.then_inc(y_ready, 1)

            in_pairs(pe, BLOCKS, step)

        @block.vector
        def _(dve):
            def step(k, s):
                j = k * 2 + s
                dve.wait_ge(y_ready, j + 1)
                xb = m.X[:, ds(j * BT, BT), :]
                nc.vector.tensor_tensor(xb, yp[:, s, :, :], xb, ALU.add).then_inc(x_ready, 1)

            in_pairs(dve, BLOCKS, step)


def build(nc, io, debug=None):
    with ExitStack() as st:
        def sb(name, shape, dt):
            return st.enter_context(nc.sbuf_tensor(name, shape, dt))

        def dram(name, shape, dt):
            return nc.dram_tensor(name, shape, dt, kind="Internal").ap()

        m = Core()
        m.X = sb("X", [P, TILES, D], F32)
        m.ident_f = sb("ident_f", [P, P], F32)
        m.ident_b = sb("ident_b", [P, P], BF16)
        m.ones_b = sb("ones_b", [P, P], BF16)
        m.before = sb("before", [P, P], BF16)
        m.maskneg = sb("maskneg", [P, WIN], F32)
        m.neghalf = sb("neghalf", [P, TILES], F32)
        m.rank = sb("rank", [P, TILES, EXPERTS], F32)
        m.hgate = sb("hgate", [P, TILES], F32)
        m.slot_get = sb("slot_get", [P, TILES], I32)
        m.slot_put = sb("slot_put", [P, TILES], I32)
        m.XS = [dram(f"slots{n}", (TOKENS, D), F32) for n in range(2)]
        m.YS = [dram(f"made{n}", (TOKENS, D), F32) for n in range(2)]
        m.QK = [dram(n, (BATCH, PARTS, D, SEQ), BF16) for n in ("q_parts", "k_parts")]
        m.V = dram("values", (GROUPS, SEQ, GF), F32)
        m.MAXROWS = [dram("max_early", (PARTS, GH * EARLY_T, P), BF16),
                     dram("max_late", (PARTS, GH * (QT - EARLY_T), P), BF16)]
        constants(nc, m, io)
        for layer in range(2):
            with nc.sbuf_tensor(f"rows{layer}", [P, TILES, D], F32) as rows:
                m.ROWS = rows
                route(nc, m, f"r{layer}", m.XS[layer], io)
                experts(nc, m, f"x{layer}", m.XS[layer], m.YS[layer], io)
                combine(nc, m, f"c{layer}", m.YS[layer], io, layer == 1)
            if layer == 0:
                project(nc, m, io)
                with nc.sbuf_tensor("AT", [P, GROUPS * QT, GF], F32) as at:
                    m.AT = at
                    attend(nc, m)
                    output(nc, m, io)


def kernel(**inputs):
    import numpy as np
    import concourse.bacc as bacc
    from concourse.bass_utils import run_bass_kernel_spmd

    def get(name):
        return np.asarray(inputs[name])

    wkv = get("L0_attn_Wkv")
    arrays = {
        "x": get("L0_attn_x").reshape(TOKENS, D),
        "wq_t": get("L0_attn_Wq").T,
        "wk_t": wkv[:D].T,
        "wv_t": wkv[D:].T,
        "wo_t": get("L0_attn_Wo").T,
        "wg": get("L0_ffn_wg"),
        "w_t": get("L0_ffn_W").transpose(0, 2, 1),
        "b": get("L0_ffn_b"),
    }
    arrays = {n: np.ascontiguousarray(a) for n, a in arrays.items()}
    nc = bacc.Bacc("TRN2", target_bir_lowering=False, num_devices=1)
    io = {n: nc.dram_tensor(n, a.shape, mybir.dt.from_np(a.dtype), kind="ExternalInput").ap()
          for n, a in arrays.items()}
    io["out"] = nc.dram_tensor("out", (TOKENS, D), F32, kind="ExternalOutput").ap()
    build(nc, io)
    r = run_bass_kernel_spmd(nc, [arrays], core_ids=[0])
    return r.results[0]["out"].reshape(BATCH, SEQ, D)
```

```python
from contextlib import ExitStack

import concourse.bass as bass
from concourse import mybir

P = 128
BATCH, SEQ, D = 2, 2048, 256
HEADS, EXPERTS = 16, 8
DH = D // HEADS
TOKENS = BATCH * SEQ
TILES = TOKENS // P
CAP = TOKENS // EXPERTS
KC = D // P
BT = 4
BLOCK = BT * P
BLOCKS = TOKENS // BLOCK
LN_EPS = 1e-5
DEN_EPS = 1e-8
SCALE = DH ** -0.5
NEG = -3.0e38

GH = 4
GROUPS = BATCH * HEADS // GH
GF = GH * DH
PARTS = 3
ROWS = 6 * DH
AROWS = ROWS + PARTS
WIN = 512
WINS = SEQ // WIN
QT = SEQ // P
UNITS = [(w, kb) for w in range(WINS) for kb in range((w + 1) * WIN // P)]
NU = len(UNITS)
ERING = 4
CHUNKS = [(t, h, c, min(WIN, (t + 1) * P - c * WIN))
          for t in range(QT) for h in range(GH) for c in range(t // BT + 1)]
NC_ = len(CHUNKS)
EARLY_T = 12
EARLY_CHUNKS = sum(1 for c in CHUNKS if c[0] < EARLY_T)
RING = 3
EARLY_JOB = EARLY_CHUNKS + 6
ROW = D + 2
NOBODY = 1 << 24

ALU = mybir.AluOpType
ACT = mybir.ActivationFunctionType
AX = mybir.AxisListType
F32 = mybir.dt.float32
BF16 = mybir.dt.bfloat16
I32 = mybir.dt.int32
ds = bass.ds


class Core:
    pass


def sems(nc, stack, *names):
    return [stack.enter_context(nc.semaphore(n)) for n in names]


def in_pairs(eng, count, body):
    for s in range(2):
        body(0, s)
    with eng.Fori(1, count // 2) as k:
        for s in range(2):
            body(k, s)


def wait_free(eng, sem, value):
    if not isinstance(value, int) or value:
        eng.wait_ge(sem, value)


def wait_alone(eng, sem, value, passed):
    eng.wait_ge(sem, value)
    eng.sem_inc(passed, 1)


def constants(nc, m, io):
    with ExitStack() as st:
        empty = st.enter_context(nc.sbuf_tensor("empty", [P, TILES // 4, ROW], F32))
        made, zeroed, stored, ones_made = sems(nc, st, "c_made", "c_zeroed", "c_stored", "c_ones")
        block = st.enter_context(nc.Block())
        per = P * (TILES // 4)

        @block.sync
        def _(sp):
            sp.dma_start(m.X[:, :, :], io["x"].rearrange("(i p) d -> p i d", p=P)).then_inc(stored, 16)
            sp.wait_ge(zeroed, 2)
            for xs in m.XS:
                for k in range(4):
                    sp.dma_start(xs[k * per:(k + 1) * per, :].rearrange("(p a) d -> p (a d)", p=P),
                                 empty[:, :, :].rearrange("p a d -> p (a d)")).then_inc(stored, 16)

        @block.scalar
        def _(act):
            act.dma_start(m.SUM.rearrange("(p a) d -> p (a d)", p=P), io["x"].rearrange("(p a) d -> p (a d)", p=P))\
                .then_inc(stored, 16)
            act.wait_ge(stored, (2 * 4 + 2) * 16)

        @block.vector
        def _(dve):
            nc.vector.memset(empty[:, :, 0:D], 0.0).then_inc(zeroed, 1)
            nc.vector.memset(empty[:, :, D:ROW].bitcast(I32), NOBODY).then_inc(zeroed, 1)
            nc.vector.memset(m.ones_b[:, :], 1.0).then_inc(ones_made, 1)
            nc.vector.memset(m.neghalf[:, :], -0.5).then_inc(ones_made, 1)

        @block.gpsimd
        def _(pool):
            nc.gpsimd.memset(m.ident_f[:, :], 0.0).then_inc(made, 1)
            nc.gpsimd.memset(m.ident_b[:, :], 0.0).then_inc(made, 1)
            nc.gpsimd.memset(m.before[:, :], 1.0).then_inc(made, 1)
            nc.gpsimd.memset(m.maskneg[:, :], 0.0).then_inc(made, 1)
            pool.wait_ge(made, 4)
            nc.gpsimd.affine_select(out=m.ident_f[:, :], in_=m.ident_f[:, :], compare_op=ALU.not_equal, fill=1.0,
                                    base=0, pattern=[[-1, P]], channel_multiplier=1).then_inc(made, 1)
            nc.gpsimd.affine_select(out=m.ident_b[:, :], in_=m.ident_b[:, :], compare_op=ALU.not_equal, fill=1.0,
                                    base=0, pattern=[[-1, P]], channel_multiplier=1).then_inc(made, 1)
            nc.gpsimd.affine_select(out=m.before[:, :], in_=m.before[:, :], compare_op=ALU.is_gt, fill=0.0,
                                    base=0, pattern=[[1, P]], channel_multiplier=-1).then_inc(made, 1)
            nc.gpsimd.affine_select(out=m.maskneg[:, :], in_=m.maskneg[:, :], compare_op=ALU.is_ge, fill=NEG,
                                    base=WIN - P, pattern=[[-1, WIN]], channel_multiplier=1).then_inc(made, 1)
            for e in range(EXPERTS):
                nc.gpsimd.memset(m.rank[:, :, e:e + 1], float(EXPERTS - e)).then_inc(made, 1)


class Moments:

    def __init__(self, nc, stack, tag, m, rounds):
        def sb(name, shape):
            return stack.enter_context(nc.sbuf_tensor(f"{tag}_{name}", shape, F32))

        self.nc, self.m, self.n = nc, m, TILES // rounds
        self.stats = sb("stats", [P, TILES, 6])
        self.work = sb("work", [P, 4, TILES])
        self.mean, self.var_eps, self.rstd = (sb(n, [P, TILES]) for n in ("mean", "var_eps", "rstd"))
        self.st_done, self.sum_done, self.step, self.var_done, self.rstd_done = sems(
            nc, stack, *(f"{tag}_{n}" for n in ("st_done", "sum_done", "mo_step", "var_done", "rstd_done")))

    def vector(self, dve, r):
        nc, at = self.nc, slice(r * self.n, (r + 1) * self.n)
        a, b, c, d = (self.work[:, n, at] for n in range(4))
        for i in range(at.start, at.stop):
            nc.vector.bn_stats(self.stats[:, i, :], self.m.X[:, i, :]).then_inc(self.st_done, 1)
        dve.wait_ge(self.st_done, at.stop)
        mean0, m20, mean1, m21 = (self.stats[:, at, n] for n in (1, 2, 4, 5))
        nc.vector.tensor_tensor(a, mean0, mean1, ALU.add).then_inc(self.sum_done, 1)
        nc.vector.tensor_tensor(b, mean0, mean1, ALU.subtract).then_inc(self.sum_done, 1)
        nc.vector.tensor_tensor(c, m20, m21, ALU.add).then_inc(self.sum_done, 1)
        dve.wait_ge(self.sum_done, 3 * r + 3)
        nc.vector.tensor_scalar(self.mean[:, at], a, 0.5, None, ALU.mult).then_inc(self.step, 1)
        nc.vector.scalar_tensor_tensor(out=d, in0=b, scalar=0.25, in1=b, op0=ALU.mult, op1=ALU.mult)\
            .then_inc(self.step, 1)
        dve.wait_ge(self.step, 3 * r + 2)
        nc.vector.scalar_tensor_tensor(out=a, in0=c, scalar=1.0 / D, in1=d, op0=ALU.mult, op1=ALU.add)\
            .then_inc(self.step, 1)
        dve.wait_ge(self.step, 3 * r + 3)
        nc.vector.tensor_scalar(self.var_eps[:, at], a, LN_EPS, None, ALU.add).then_inc(self.var_done, 1)

    def gpsimd(self, pool, r):
        at = slice(r * self.n, (r + 1) * self.n)
        pool.wait_ge(self.var_done, r + 1)
        self.nc.gpsimd.tensor_tensor(self.rstd[:, at], self.var_eps[:, at], self.m.neghalf[:, at], ALU.pow)\
            .then_inc(self.rstd_done, 1)

    def normalise(self, out, i):
        return self.nc.vector.tensor_scalar(out, self.m.X[:, ds(i, 1), :].rearrange("p o d -> p (o d)"),
                                            self.mean[:, ds(i, 1)], self.rstd[:, ds(i, 1)], ALU.subtract, ALU.mult)


def moe(nc, m, tag, xs, target, io, last_layer):
    ROUNDS = 4
    RT = TILES // ROUNDS
    RE = RT * EXPERTS
    with ExitStack() as st:
        def sb(name, shape, dt):
            return st.enter_context(nc.sbuf_tensor(f"{tag}_{name}", shape, dt))

        def sem(*names):
            return sems(nc, st, *(f"{tag}_{n}" for n in names))

        mo = Moments(nc, st, tag, m, ROUNDS)
        rows = sb("rows", [P, TILES, ROW], F32)
        xt = sb("xt", [P, 2, 2, KC, BLOCK], F32)
        wg = sb("wg", [P, KC, EXPERTS], F32)
        z, ez, pick, ranked, at = (sb(n, [P, ROUNDS, RT, EXPERTS], F32) for n in ("z", "ez", "pick", "ranked", "at"))
        mask = sb("mask", [P, ROUNDS, RT, EXPERTS], BF16)
        before = sb("count", [P, ROUNDS + 1, EXPERTS], F32)
        lmax, se, gate, cm, loc, keep, locc, base, slotf, drop = (
            sb(n, [P, ROUNDS, RT], F32) for n in
            ("lmax", "se", "gate", "cm", "loc", "keep", "locc", "base", "slotf", "drop"))
        slot = sb("slot", [P, TILES], I32)
        weights = sb("we", [P, EXPERTS, KC, D], F32)
        bias = sb("be", [P, EXPERTS, D], F32)
        xe = sb("xe", [P, 2, BT, ROW], F32)
        marks = sb("marks", [P, 2, BT, 2], F32)
        xet = sb("xet", [P, 2, KC, BLOCK], F32)
        ye = sb("ye", [P, 2, BT, D], F32)
        xtp = st.enter_context(nc.psum_tensor(f"{tag}_xtp", [P, 2, KC, BLOCK], F32))
        pos = st.enter_context(nc.psum_tensor(f"{tag}_pos", [P, ROUNDS, P], F32))
        yp = st.enter_context(nc.psum_tensor(f"{tag}_yp", [P, 2, 2 * D], F32))
        lgp = st.enter_context(nc.psum_tensor(f"{tag}_lg", [P, 2 * D], F32))
        lg = [lgp[:, 0:RE], yp[:, 0, 0:RE]]
        (wg_loaded, counted, numbered, xn_ready, xtp_ready, xt_ready, lg_ready, chain, z_ready, ez_ready,
         mask_ready, pos_ready, slot_ready, scattered, w_loaded, xe_in0, xe_in1, xetp_ready, xet_ready, yp_ready,
         yp_read, ye_ready, marks_ready, added0, added1, x_stored, passed) = sem(
            "wg_loaded", "counted", "numbered", "xn_ready", "xtp_ready", "xt_ready", "lg_ready", "chain", "z_ready",
            "ez_ready", "mask_ready", "pos_ready", "slot_ready", "scattered", "w_loaded", "xe_in0", "xe_in1",
            "xetp_ready", "xet_ready", "yp_ready", "yp_read", "ye_ready", "marks_ready", "added0", "added1",
            "x_stored", "passed")
        xe_in, added = (xe_in0, xe_in1), (added0, added1)
        block = st.enter_context(nc.Block())

        @block.sync
        def _(sp):
            sp.dma_start(wg[:, :, :], io["wg"].rearrange("(c p) e -> p c e", p=P)).then_inc(wg_loaded, 16)
            if last_layer:
                sp.dma_start(target.rearrange("(i p) d -> p i d", p=P), m.X[:, :, :]).then_inc(x_stored, 16)
            sp.wait_ge(scattered, 16 * TILES)

            def step(k, s):
                wait_free(sp, xetp_ready, k * 2)
                wait_free(sp, marks_ready, k * 2)
                sp.dma_start(xe[:, s, :, :], xs[ds((k * 2 + s) * CAP, CAP), :].rearrange("(t p) d -> p t d", p=P))\
                    .then_inc(xe_in[s], 16)

            in_pairs(sp, EXPERTS, step)

        @block.vector
        def _(dve):
            steps = [0]

            def link(ins):
                steps[0] += 1
                ins.then_inc(chain, 1)
                dve.wait_ge(chain, steps[0])

            def normalise(r):
                dve.wait_ge(mo.rstd_done, r + 1)
                for i in range(r * RT, (r + 1) * RT):
                    mo.normalise(rows[:, i, 0:D], i).then_inc(xn_ready, 1)

            def route(r):
                def wide(a):
                    return a[:, r, :].unsqueeze(2).to_broadcast([P, RT, EXPERTS])

                tiles = slice(r * RT, (r + 1) * RT)
                dve.wait_ge(lg_ready, r + 1)
                logits = lg[r % 2].rearrange("p (i e) -> p i e", e=EXPERTS)
                link(nc.vector.tensor_reduce(lmax[:, r, :], logits, AX.X, ALU.max))
                nc.vector.tensor_tensor(z[:, r, :, :], logits, wide(lmax), ALU.subtract).then_inc(z_ready, 1)
                dve.wait_ge(z_ready, r + 1)
                link(nc.vector.tensor_scalar(pick[:, r, :, :], z[:, r, :, :], 0.0, None, ALU.is_ge))
                link(nc.vector.tensor_tensor(ranked[:, r, :, :], pick[:, r, :, :], m.rank[:, 0:RT, :], ALU.mult))
                link(nc.vector.tensor_reduce(cm[:, r, :], ranked[:, r, :, :], AX.X, ALU.max))
                nc.vector.tensor_tensor(mask[:, r, :, :], ranked[:, r, :, :], wide(cm), ALU.is_equal)\
                    .then_inc(mask_ready, 1)
                dve.wait_ge(ez_ready, r + 1)
                link(nc.vector.tensor_reduce(se[:, r, :], ez[:, r, :, :], AX.X, ALU.add))
                link(nc.vector.reciprocal(gate[:, r, :], se[:, r, :]))
                link(nc.vector.tensor_scalar(base[:, r, :], cm[:, r, :], -float(CAP), float(CAP * EXPERTS),
                                             ALU.mult, ALU.add))
                dve.wait_ge(pos_ready, r + 1)
                dve.wait_ge(mask_ready, r + 1)
                counts = pos[:, r, 0:RE].rearrange("p (i e) -> p i e", e=EXPERTS)
                link(nc.vector.tensor_tensor(at[:, r, :, :], counts,
                                             before[:, r:r + 1, :].to_broadcast([P, RT, EXPERTS]), ALU.add))
                link(nc.vector.tensor_tensor(before[:, r + 1, :], pos[:, r, RE:RE + EXPERTS], before[:, r, :],
                                             ALU.add))
                link(nc.vector.tensor_tensor(pick[:, r, :, :], at[:, r, :, :], mask[:, r, :, :], ALU.mult))
                link(nc.vector.tensor_reduce(loc[:, r, :], pick[:, r, :, :], AX.X, ALU.add))
                link(nc.vector.tensor_scalar(keep[:, r, :], loc[:, r, :], float(CAP), None, ALU.is_lt))
                link(nc.vector.scalar_tensor_tensor(out=rows[:, tiles, D + 1], in0=gate[:, r, :], scalar=0.5,
                                                    in1=keep[:, r, :], op0=ALU.mult, op1=ALU.mult))
                link(nc.vector.tensor_tensor(slotf[:, r, :], base[:, r, :], loc[:, r, :], ALU.add))
                link(nc.vector.tensor_scalar(drop[:, r, :], keep[:, r, :], -2.0 * TOKENS, 2.0 * TOKENS,
                                             ALU.mult, ALU.add))
                nc.vector.tensor_tensor(slot[:, tiles], slotf[:, r, :], drop[:, r, :], ALU.add)\
                    .then_inc(slot_ready, 1)

            nc.vector.memset(before[:, 0, :], 0.0).then_inc(counted, 1)
            dve.wait_ge(counted, 1)
            mo.vector(dve, 0)
            for r in range(ROUNDS):
                if r + 1 < ROUNDS:
                    mo.vector(dve, r + 1)
                normalise(r)
                if r:
                    route(r - 1)
            route(ROUNDS - 1)

            dve.wait_ge(w_loaded, 32)

            def step(k, s):
                e = k * 2 + s
                dve.wait_ge(xe_in[s], k * 16 + 16)
                wait_free(dve, added[s], k * (16 * BT))
                nc.vector.tensor_copy(marks[:, s, :, :], xe[:, s, :, D:ROW]).then_inc(marks_ready, 1)
                for u in range(2):
                    dve.wait_ge(yp_ready, e * 2 + (u + 1))
                    pair = ye[:, s, 2 * u:2 * u + 2, :]
                    nc.vector.tensor_tensor(pair, yp[:, u, :].rearrange("p (t d) -> p t d", d=D),
                                            bias[:, ds(e, 1), :].to_broadcast([P, 2, D]), ALU.add).then_inc(yp_read, 1)
                    if u == 0:
                        dve.wait_ge(marks_ready, e + 1)
                    dve.wait_ge(yp_read, e * 2 + (u + 1))
                    for t in range(2 * u, 2 * u + 2):
                        nc.vector.tensor_scalar(ye[:, s, t, :], ye[:, s, t, :], marks[:, s, t, 1:2], None, ALU.mult)\
                            .then_inc(ye_ready, 1)

            in_pairs(dve, EXPERTS, step)

        @block.gpsimd
        def _(pool):
            nc.gpsimd.iota(rows[:, :, D].bitcast(I32), pattern=[[P, TILES]], base=0, channel_multiplier=1)\
                .then_inc(numbered, 1)
            pool.wait_ge(numbered, 1)

            def scatter(r):
                pool.wait_ge(slot_ready, r + 1)
                for i in range(r * RT, (r + 1) * RT):
                    nc.gpsimd.indirect_dma_start(
                        out=xs[:, :], out_offset=bass.IndirectOffsetOnAxis(ap=slot[:, i:i + 1], axis=0),
                        in_=rows[:, i, :], in_offset=None, bounds_check=TOKENS - 1,
                        oob_is_err=False).then_inc(scattered, 16)

            mo.gpsimd(pool, 0)
            mo.gpsimd(pool, 1)
            for r in range(ROUNDS):
                if r + 2 < ROUNDS:
                    mo.gpsimd(pool, r + 2)
                scatter(r)
            if last_layer:
                pool.wait_ge(x_stored, 16)

            def step(k, s):
                for t in range(BT):
                    wait_alone(pool, ye_ready, (k * 2 + s) * BT + (t + 1), passed)
                    nc.gpsimd.indirect_dma_start(
                        out=target, out_offset=bass.IndirectOffsetOnAxis(ap=marks[:, s, t, 0:1].bitcast(I32), axis=0),
                        in_=ye[:, s, t, :], in_offset=None, bounds_check=TOKENS - 1, oob_is_err=False,
                        compute_op=ALU.add).then_inc(added[s], 16)

            in_pairs(pool, EXPERTS, step)
            for s in range(2):
                pool.wait_ge(added[s], EXPERTS // 2 * BT * 16)

        @block.scalar
        def _(act):
            act.dma_start(weights[:, :, :, :], io["w_t"].rearrange("e (c p) f -> p e c f", p=P)).then_inc(w_loaded, 16)
            act.dma_start(bias[:, :, :], io["b"].unsqueeze(0).to_broadcast([P, EXPERTS, D])).then_inc(w_loaded, 16)

            def exps(r):
                act.wait_ge(z_ready, r + 1)
                nc.scalar.activation(ez[:, r, :, :], z[:, r, :, :], ACT.Exp).then_inc(ez_ready, 1)

            for r in range(ROUNDS):
                for b in range(2):
                    act.wait_ge(xtp_ready, 2 * r + b + 1)
                    if r >= 2:
                        act.wait_ge(lg_ready, r - 1)
                    nc.scalar.activation(xt[:, r % 2, b, :, :], xtp[:, b, :, :], ACT.Copy).then_inc(xt_ready, 1)
                if r:
                    exps(r - 1)
            exps(ROUNDS - 1)

            def step(k, s):
                act.wait_ge(xetp_ready, k * 2 + s + 1)
                wait_free(act, yp_ready, k * 4)
                nc.scalar.activation(xet[:, s, :, :], xtp[:, s, :, :], ACT.Copy).then_inc(xet_ready, 1)

            in_pairs(act, EXPERTS, step)

        @block.tensor
        def _(pe):
            def logits(r):
                for b in range(2):
                    for t in range(BT):
                        i = 2 * BT * r + b * BT + t
                        if t == 0:
                            pe.wait_ge(xn_ready, i + BT)
                            if r:
                                pe.wait_ge(xt_ready, 2 * r - 1 + b)
                        for c in range(KC):
                            last = pe.transpose(xtp[:, b, c, t * P:(t + 1) * P], rows[:, i, c * P:(c + 1) * P],
                                                m.ident_f[:, :])
                    last.then_inc(xtp_ready, 1)
                for b in range(2):
                    pe.wait_ge(xt_ready, 2 * r + b + 1)
                    for t in range(BT):
                        i = b * BT + t
                        for c in range(KC):
                            last = pe.matmul(lg[r % 2][:, i * EXPERTS:(i + 1) * EXPERTS], xt[:, r % 2, b, c, t * P:(t + 1) * P],
                                             wg[:, c, :], start=(c == 0), stop=(c == KC - 1))
                last.then_inc(lg_ready, 1)

            def count(r):
                pe.wait_ge(mask_ready, r + 1)
                pe.matmul(pos[:, r, 0:RE], m.before[:, :], mask[:, r, :, :].rearrange("p i e -> p (i e)"),
                          start=True, stop=False)
                for i in range(RT - 1):
                    later = RT - 1 - i
                    pe.matmul(pos[:, r, (i + 1) * EXPERTS:RE].rearrange("p (i e) -> p i e", e=EXPERTS), m.ones_b[:, :],
                              mask[:, r, i:i + 1, :].to_broadcast([P, later, EXPERTS]), start=False,
                              stop=(i == RT - 2))
                for i in range(RT):
                    last = pe.matmul(pos[:, r, RE:RE + EXPERTS], m.ones_b[:, :], mask[:, r, i, :], start=(i == 0),
                                     stop=(i == RT - 1))
                last.then_inc(pos_ready, 1)

            pe.wait_ge(wg_loaded, 16)
            for r in range(ROUNDS):
                logits(r)
                if r:
                    count(r - 1)
            count(ROUNDS - 1)

            pe.wait_ge(w_loaded, 32)
            pe.wait_ge(xt_ready, 2 * ROUNDS)

            def step(k, s):
                e = k * 2 + s
                pe.wait_ge(xe_in[s], k * 16 + 16)
                wait_free(pe, xet_ready, k * 2)
                for c in range(KC):
                    for t in range(BT):
                        last = pe.transpose(xtp[:, s, c, t * P:(t + 1) * P], xe[:, s, t, c * P:(c + 1) * P],
                                            m.ident_f[:, :])
                last.then_inc(xetp_ready, 1)
                pe.wait_ge(xet_ready, e + 1)
                for u in range(2):
                    if not isinstance(e, int) or e:
                        pe.wait_ge(yp_read, e * 2 + (u - 1))
                    for t in range(2):
                        for c in range(KC):
                            tok = (2 * u + t) * P
                            last = pe.matmul(yp[:, u, t * D:(t + 1) * D], xet[:, s, c, tok:tok + P],
                                             weights[:, ds(e, 1), c, :], start=(c == 0), stop=(c == KC - 1))
                    last.then_inc(yp_ready, 1)

            in_pairs(pe, EXPERTS, step)


def project(nc, m, io):
    ROUNDS = 4
    with ExitStack() as st:
        def sb(name, shape, dt):
            return st.enter_context(nc.sbuf_tensor(f"pr_{name}", shape, dt))

        mo = Moments(nc, st, "pr", m, ROUNDS)
        ring = sb("ring", [P, 2, BT, D], F32)
        xt = sb("xt", [P, 2, KC, BLOCK], F32)
        w = sb("w", [P, 3, KC, D], F32)
        parts = sb("parts", [P, 2, 2, PARTS, KC * BLOCK], BF16)
        rest = sb("rest", [P, 2, 2, KC * BLOCK], F32)
        vals = sb("vals", [P, 2, BT, D], F32)
        xtp = st.enter_context(nc.psum_tensor("pr_xtp", [P, KC, BLOCK], F32))
        qkp = [st.enter_context(nc.psum_tensor(f"pr_{n}p", [P, KC * BLOCK], F32)) for n in "qk"]
        vp = st.enter_context(nc.psum_tensor("pr_vp", [P, BT, D], F32))
        (w_loaded, xn_ready, xtp_ready, xt_ready, v_ready, v_out, stored0, stored1, filled) = sems(
            nc, st, *(f"pr_{n}" for n in ("w_loaded", "xn_ready", "xtp_ready", "xt_ready", "v_ready", "v_out",
                                          "stored0", "stored1", "filled")))
        x_in = sems(nc, st, *(f"pr_x_in{r}" for r in range(ROUNDS)))
        qk_ready = sems(nc, st, "pr_q_ready", "pr_k_ready")
        part1 = sems(nc, st, "pr_q_part1", "pr_k_part1")
        rest1 = sems(nc, st, "pr_q_rest", "pr_k_rest")
        part2 = sems(nc, st, "pr_q_part2", "pr_k_part2")
        part3 = sems(nc, st, "pr_q_part3", "pr_k_part3")
        stored = (stored0, stored1)
        dmas = 3
        scale = (SCALE, 1.0)
        block = st.enter_context(nc.Block())

        @block.vector
        def _(dve):
            for r in range(ROUNDS):
                dve.wait_ge(x_in[r], 16)
                mo.vector(dve, r)
            dve.wait_ge(mo.rstd_done, ROUNDS)

            def step(k, s):
                j = k * 2 + s
                wait_free(dve, xtp_ready, k * 2)
                for t in range(BT):
                    mo.normalise(ring[:, s, t, :], j * BT + t).then_inc(xn_ready, 1)
                wait_free(dve, stored[s], k * (dmas * 16))
                for n in range(2):
                    first, second, third = (parts[:, s, n, c, :] for c in range(PARTS))
                    dve.wait_ge(qk_ready[n], j + 1)
                    dve.wait_ge(part1[n], j + 1)
                    nc.vector.scalar_tensor_tensor(out=rest[:, s, n, :], in0=qkp[n][:, :], scalar=scale[n], in1=first,
                                                   op0=ALU.mult, op1=ALU.subtract).then_inc(rest1[n], 1)
                    dve.wait_ge(rest1[n], j + 1)
                    nc.vector.tensor_copy(second, rest[:, s, n, :]).then_inc(part2[n], 1)
                    dve.wait_ge(part2[n], j + 1)
                    nc.vector.tensor_tensor(third, rest[:, s, n, :], second, ALU.subtract).then_inc(part3[n], 1)

            in_pairs(dve, BLOCKS, step)

        @block.gpsimd
        def _(pool):
            for n, fill in enumerate([(m.K[s][ROWS:AROWS, :, :, :], 1.0) for s in range(2)]
                                     + [(m.V[s][:, :, DH:2 * DH], 1.0) for s in range(2)]
                                     + [(m.part_max[s][:, :, :], NEG) for s in range(2)]):
                if n:
                    pool.wait_ge(filled, n)
                nc.gpsimd.memset(*fill).then_inc(filled, 1)
            for r in range(ROUNDS):
                mo.gpsimd(pool, r)

        @block.scalar
        def _(act):
            def step(k, s):
                j = k * 2 + s
                act.wait_ge(xtp_ready, j + 1)
                wait_free(act, v_ready, k * 2)
                nc.scalar.activation(xt[:, s, :, :], xtp[:, :, :], ACT.Copy).then_inc(xt_ready, 1)
                wait_free(act, stored[s], k * (dmas * 16))
                for n in range(2):
                    act.wait_ge(qk_ready[n], j + 1)
                    nc.scalar.activation(parts[:, s, n, 0, :], qkp[n][:, :], ACT.Copy, scale=scale[n])\
                        .then_inc(part1[n], 1)
                act.wait_ge(v_ready, j + 1)
                nc.scalar.activation(vals[:, s, :, :], vp[:, :, :], ACT.Copy).then_inc(v_out, 1)

            in_pairs(act, BLOCKS, step)

        @block.tensor
        def _(pe):
            pe.wait_ge(w_loaded, 16 * 3)

            def step(k, s):
                j = k * 2 + s
                pe.wait_ge(xn_ready, j * BT + BT)
                wait_free(pe, xt_ready, j)
                for c in range(KC):
                    for t in range(BT):
                        last = pe.transpose(xtp[:, c, t * P:(t + 1) * P], ring[:, s, t, c * P:(c + 1) * P],
                                            m.ident_f[:, :])
                last.then_inc(xtp_ready, 1)
                pe.wait_ge(xt_ready, j + 1)
                for n in range(2):
                    wait_free(pe, rest1[n], j)
                    for co in range(KC):
                        for c in range(KC):
                            last = pe.matmul(qkp[n][:, co * BLOCK:(co + 1) * BLOCK], w[:, n, c, co * P:(co + 1) * P],
                                             xt[:, s, c, :], start=(c == 0), stop=(c == KC - 1))
                    last.then_inc(qk_ready[n], 1)
                wait_free(pe, v_out, j)
                for t in range(BT):
                    for c in range(KC):
                        last = pe.matmul(vp[:, t, :], xt[:, s, c, t * P:(t + 1) * P], w[:, 2, c, :],
                                         start=(c == 0), stop=(c == KC - 1))
                last.then_inc(v_ready, 1)

            in_pairs(pe, BLOCKS, step)

        @block.sync
        def _(sp):
            per = TOKENS // ROUNDS
            for r in range(ROUNDS):
                sp.dma_start(m.X[:, r * TILES // ROUNDS:(r + 1) * TILES // ROUNDS, :],
                             m.SUM[r * per:(r + 1) * per, :].rearrange("(i p) d -> p i d", p=P)).then_inc(x_in[r], 16)
            for n, name in enumerate(("wq_t", "wk_t", "wv_t")):
                sp.dma_start(w[:, n, :, :], io[name].rearrange("(c p) f -> p c f", p=P)).then_inc(w_loaded, 16)
            with sp.Fori(0, BLOCKS // 2) as k:
                for s in range(2):
                    j = k * 2 + s
                    for n in range(2):
                        sp.wait_ge(part3[n], j + 1)
                        sp.dma_start(m.QK[n][ds(j, 1), :, :].rearrange("o (x p) t -> p (o x) t", p=P),
                                     parts[:, s, n, :, :].rearrange("p a (c t) -> p (a c) t", c=KC))\
                            .then_inc(stored[s], 16)
                    sp.wait_ge(v_out, j + 1)
                    sp.dma_start(m.VALUES[ds(j * BT, BT), :, :].rearrange("t p f -> p t f"), vals[:, s, :, :])\
                        .then_inc(stored[s], 16)
            for s in range(2):
                sp.wait_ge(stored[s], BLOCKS // 2 * dmas * 16)


def attend(nc, m):
    with ExitStack() as st:
        def sb(name, shape, dt):
            return st.enter_context(nc.sbuf_tensor(f"at_{name}", shape, dt))

        def ps(name, shape, dt=F32):
            return st.enter_context(nc.psum_tensor(f"at_{name}", shape, dt))

        Q, K, V, part_max = m.Q, m.K, m.V, m.part_max
        v_raw = sb("vr", [P, QT, GF], F32)
        ex = [sb(f"e{r}", [P, GH, WIN], F32) for r in range(ERING)]
        neg_max = sb("nm", [P, GH * QT], F32)
        left = sb("left", [P, GH * QT], F32)
        max_parts = sb("mp", [P, PARTS, GH * QT], BF16)
        max_rows = sb("mr", [GH * EARLY_T, PARTS, P], BF16)
        junk = sb("junk", [P, RING, WIN], BF16)
        osb = sb("osb", [P, WIN], F32)
        den = sb("den", [P, 2, BT * GH], F32)
        score = [ps(f"s{h}", [P, 2, WIN]) for h in range(2)]
        bank = [ps(f"b{r}", [P, WIN]) for r in range(RING)]
        sums = ps("o", [P, WIN])

        (scores_ready, exp_done, pv_done, masked, job_ready, job_read, max_step, rows_ready, rows_stored, rows_early,
         rows_late, o_out, norm_step, v_in, v_laid, passed) = sems(nc, st, *(f"at_{n}" for n in (
             "scores_ready", "exp_done", "pv_done", "masked", "job_ready", "job_read", "max_step", "rows_ready",
             "rows_stored", "rows_early", "rows_late", "o_out", "norm_step", "v_in", "v_laid", "passed")))
        quarter = [sems(nc, st, *(f"at_in{s}_{w}" for w in range(WINS))) for s in range(2)]
        block = st.enter_context(nc.Block())

        QROWS = [(0, 3, 0, 0), (3, 2, 1, 0), (5, 1, 2, 0)]
        KROWS = [(0, 3, 0, 1), (3, 2, 0, 1), (5, 1, 0, 0)]
        qdmas = len(QROWS) + len(KROWS)
        DIAG = sum(1 for w, kb in UNITS if kb * P >= w * WIN)
        first_unit = [n for n, (w, kb) in enumerate(UNITS) if kb == 0]

        jobs = [[] for _ in range(NU)]
        for k in range(NC_):
            jobs[1 + k * (NU - 2) // NC_].append(("chunk", k))
        early_unit = next(n for n in range(NU) if ("chunk", EARLY_CHUNKS - 1) in jobs[n])
        SPLIT_LATE, SPLIT_EARLY = 1, early_unit + 1
        jobs[SPLIT_LATE + 2].append(("rows", False))
        jobs[SPLIT_EARLY + 2].append(("rows", True))
        for w in range(WINS - 1):
            jobs[first_unit[w + 1] + 3].append(("window", w))
        jobs.append([("window", WINS - 1)])

        def listed(nxt):
            number, out = 0, []
            for unit in jobs:
                kept = [j for j in unit if nxt or j[0] == "window" or j == ("rows", False)]
                out.append([(number + k, *j) for k, j in enumerate(kept)])
                number += len(kept)
            return out

        PER_GROUP = sum(len(u) for u in jobs)
        BEFORE = NC_ + 1

        def raised(g, per, plus=0):
            return g * per + (plus + 1)

        def per_group(g, per, plus=0):
            return g * per + plus

        def jobs_done(g, number):
            return number if g is None else g * PER_GROUP + (BEFORE + number)

        def groups(eng, body):
            with eng.Fori(0, GROUPS // 2 - 1) as i:
                for s in range(2):
                    body(i * 2 + s, s, True)
            body(GROUPS - 2, 0, True)
            body(GROUPS - 1, 1, False)

        @block.sync
        def _(sp):
            def load(b, hg, s, earlier):
                for w in range(WINS):
                    for buf, dram, rows in ((Q[s], m.QK[0], QROWS), (K[s], m.QK[1], KROWS)):
                        for r0, n, part, step in rows:
                            src = dram[b * WINS + w, :, :].rearrange("(c g) t -> c g t", c=PARTS)[
                                part:part + (n if step else 1), ds(hg * GF, GF), :]\
                                .rearrange("c (d h) t -> c d (h t)", h=GH)
                            if n > 1 and not step:
                                src = src.to_broadcast([n, DH, GH * WIN])
                            sp.dma_start(buf[r0 * DH:(r0 + n) * DH, w, :, :].rearrange("r h t -> r (h t)"), src)\
                                .then_inc(quarter[s][w], 16)
                if earlier is not None:
                    sp.wait_ge(v_laid, earlier)
                sp.dma_start(v_raw[:, :, :], m.VALUES[b * QT:(b + 1) * QT, :, ds(hg * GF, GF)]
                             .rearrange("k p f -> p k f")).then_inc(v_in, 16)

            def max_rows_in(g, s, early):
                w0, w1 = (0, EARLY_T // BT) if early else (EARLY_T // BT, WINS)
                dram = m.MAXROWS[0 if early else 1]
                done = per_group(g, 2, 1 if early else 2)
                if not isinstance(g, int) or g:
                    wait_alone(sp, rows_early if early else rows_late, per_group(g, 16), passed)
                wait_alone(sp, rows_ready, done, passed)
                sp.dma_start(dram.rearrange("c r x -> r c x"), max_rows[0:(w1 - w0) * GH * BT, :, :])\
                    .then_inc(rows_stored, 16)
                sp.wait_ge(rows_stored, done * 16)
                sp.dma_start(Q[s][ROWS:AROWS, w0:w1, :, :].rearrange("c w h t -> c (w h t)"),
                             dram.rearrange("c r x -> c (r x)")).then_inc(rows_early if early else rows_late, 16)

            def step(g, s, nxt, nb=None, nh=None):
                max_rows_in(g, s, False)
                if nxt:
                    max_rows_in(g + 1, 1 - s, True)
                if nb is not None:
                    sp.wait_ge(pv_done, raised(g, NU, NU))
                    load(nb, nh, s, g + 2)

            load(0, 0, 0, None)
            load(0, 1, 1, 1)
            max_rows_in(0, 0, True)
            step(0, 0, True, 0, 2)
            step(1, 1, True, 0, 3)
            with sp.Fori(1, GROUPS // 2 - 1) as i:
                for s in range(2):
                    step(i * 2 + s, s, True, 1, i * 2 - 2 + s)
            step(GROUPS - 2, 0, True)
            step(GROUPS - 1, 1, False)

        @block.gpsimd
        def _(pool):
            def lay_values(g, s):
                wait_alone(pool, v_in, per_group(g, 16, 16), passed)
                nc.gpsimd.tensor_copy(V[s][:, :, 0:DH], v_raw[:, :, :].rearrange("p k (h d) -> p (k h) d", d=DH))\
                    .then_inc(v_laid, 1)

            def step(g, s, nxt):
                for n, (w, kb) in enumerate(UNITS):
                    off = kb * P - w * WIN
                    if nxt and n == NU // 2:
                        lay_values(g + 1, 1 - s)
                    if off < 0:
                        continue
                    wait_alone(pool, exp_done, raised(g, 2 * NU, 2 * n + 2), passed)
                    tri = ex[n % ERING][:, :, off:off + P]
                    nc.gpsimd.affine_select(out=tri, in_=tri, compare_op=ALU.is_ge, fill=0.0, base=0,
                                            pattern=[[0, GH], [1, P]], channel_multiplier=-1).then_inc(masked, 1)

            lay_values(0, 0)
            groups(pool, step)

        @block.scalar
        def _(act):
            turned = [0]

            def window_out(g, w, unit, nxt):
                act.wait_ge(pv_done, raised(g, NU, unit))
                if w:
                    number = next(j[0] for u in listed(nxt) for j in u if j[1:] == ("window", w - 1))
                    act.wait_ge(job_ready, jobs_done(g, number + 1))
                else:
                    act.wait_ge(job_ready, jobs_done(g, 0))
                nc.scalar.activation(osb[:, :], sums[:, :], ACT.Copy).then_inc(o_out, 1)

            def step(g, s, nxt):
                for n, (w, kb) in enumerate(UNITS):
                    off = max(0, kb * P - w * WIN)
                    act.wait_ge(pv_done, raised(g, NU, max(0, n - ERING + 1)))
                    for half in range(2):
                        act.wait_ge(scores_ready, per_group(g, 2 * NU, 2 * n + half + 1))
                        nc.scalar.activation(ex[n % ERING][:, 2 * half:2 * half + 2, off:WIN],
                                             score[half][:, :, off:WIN], ACT.Exp).then_inc(exp_done, 1)
                    if w > 0 and kb == 0:
                        window_out(g, w - 1, n, nxt)
                window_out(g, WINS - 1, NU, nxt)

            act.sem_inc(pv_done, 1)
            groups(act, step)

        @block.vector
        def _(dve):
            def chunk(g, s, number, k):
                t, h, c, width = CHUNKS[k]
                at = ((t // BT * GH + h) * BT + t % BT)
                out = part_max[s][:, at, c:c + 1]
                src = bank[number % RING]
                if c == t // BT:
                    if number >= RING:
                        dve.wait_ge(job_read, jobs_done(g, number - RING + 1))
                    wait_alone(dve, job_ready, jobs_done(g, number + 1), passed)
                    nc.vector.tensor_tensor_reduce(
                        out=junk[:, number % RING, 0:width], in0=src[:, 0:width],
                        in1=m.maskneg[:, WIN - width:WIN], scale=1.0, scalar=NEG,
                        op0=ALU.add, op1=ALU.max, accum_out=out).then_inc(job_read, 1)
                else:
                    dve.wait_ge(job_ready, jobs_done(g, number + 1))
                    nc.vector.tensor_reduce(out, src[:, 0:width], AX.X, ALU.max).then_inc(job_read, 1)

            def split(g, s, early, read, turned):
                r0, r1 = (0, EARLY_T * GH) if early else (EARLY_T * GH, QT * GH)
                n = r1 - r0
                done = [0]
                start = per_group(g, 2 * 5, 0 if early else 5)

                def link(ins):
                    done[0] += 1
                    ins.then_inc(max_step, 1)
                    dve.wait_ge(max_step, start + done[0])

                dve.wait_ge(job_read, read)
                link(nc.vector.tensor_reduce(neg_max[:, 0:n], part_max[s][:, r0:r1, :], AX.X, ALU.max, negate=True))
                if turned is not None:
                    dve.wait_ge(job_ready, turned)
                link(nc.vector.tensor_copy(max_parts[:, 0, 0:n], neg_max[:, 0:n]))
                link(nc.vector.tensor_tensor(left[:, 0:n], neg_max[:, 0:n], max_parts[:, 0, 0:n], ALU.subtract))
                link(nc.vector.tensor_copy(max_parts[:, 1, 0:n], left[:, 0:n]))
                link(nc.vector.tensor_tensor(max_parts[:, 2, 0:n], left[:, 0:n], max_parts[:, 1, 0:n], ALU.subtract))

            def rows_out(g, number, early):
                n = GH * (EARLY_T if early else QT - EARLY_T)
                dve.wait_ge(job_ready, jobs_done(g, number + 1))
                if g is not None:
                    dve.wait_ge(rows_stored, per_group(g, 32, 32 if early else 16))
                nc.vector.tensor_copy(max_rows[0:n, :, :], bank[number % RING][0:n, 0:PARTS * P // 2].bitcast(BF16)
                                      .rearrange("r (c x) -> r c x", c=PARTS)).then_inc(rows_ready, 1)
                dve.wait_ge(rows_ready, 1 if g is None else per_group(g, 2, 3 if early else 2))
                dve.sem_inc(job_read, 1)

            def normalise(g, number, w):
                dve.wait_ge(job_ready, jobs_done(g, number + 1))
                start = per_group(g, 2 * WINS, 2 * w)
                view = bank[number % RING][:, :].rearrange("p (t h a f) -> p (t h) a f", t=BT, h=GH, a=2)
                nc.vector.tensor_scalar(den[:, 0, :], view[:, :, 1, 0:1].rearrange("p n f -> p (n f)"), DEN_EPS, None,
                                        ALU.add).then_inc(norm_step, 1)
                dve.wait_ge(norm_step, start + 1)
                nc.vector.reciprocal(den[:, 1, :], den[:, 0, :]).then_inc(norm_step, 1)
                dve.wait_ge(norm_step, start + 2)
                nc.vector.tensor_tensor(
                    m.AT[:, ds(g * QT + w * BT, BT), :].rearrange("p t (h d) -> p (t h) d", h=GH), view[:, :, 0, :],
                    den[:, 1, :].unsqueeze(2).to_broadcast([P, BT * GH, DH]), ALU.mult).then_inc(job_read, 1)

            def number_of(nxt, what):
                return next(j[0] for u in listed(nxt) for j in u if j[1:] == what)

            def step(g, s, nxt):
                for n, unit in enumerate(listed(nxt)):
                    for number, what, arg in unit:
                        if what == "chunk":
                            chunk_of = (g, 1 - s, number, arg)
                            chunk(*chunk_of)
                        elif what == "rows":
                            rows_out(g, number, arg)
                        else:
                            normalise(g, number, arg)
                    if n == SPLIT_LATE:
                        split(g, s, False, jobs_done(g, 0), jobs_done(g, 0))
                    if nxt and n == SPLIT_EARLY:
                        split(g + 1, 1 - s, True, jobs_done(g, number_of(nxt, ("chunk", EARLY_CHUNKS - 1)) + 1),
                              jobs_done(g, number_of(nxt, ("rows", False)) + 1))

            for number in range(BEFORE):
                if number < EARLY_JOB:
                    chunk(None, 0, number, number)
                elif number > EARLY_JOB:
                    chunk(None, 0, number, number - 1)
                else:
                    rows_out(None, number, True)
                if number == EARLY_JOB - 4:
                    split(0, 0, True, EARLY_CHUNKS, None)
            groups(dve, step)

        @block.tensor
        def _(pe):
            def free(g, number):
                if g is None and number < RING:
                    return
                pe.wait_ge(job_read, jobs_done(g, number - RING + 1 if number >= RING else 0))

            def chunk(g, s, number, k, visit):
                t, h, c, width = CHUNKS[k]
                w = t // BT
                if k == 0 or CHUNKS[k - 1][0] // BT != w:
                    pe.wait_ge(quarter[s][w], visit * (16 * qdmas))
                free(g, number)
                pe.matmul(bank[number % RING][:, 0:width], Q[s][0:ROWS, w, h, t % BT * P:(t % BT + 1) * P],
                          K[s][0:ROWS, c, h, 0:width], start=True, stop=True).then_inc(job_ready, 1)

            def rows(g, number, early, split_count):
                n = GH * (EARLY_T if early else QT - EARLY_T)
                free(g, number)
                wait_alone(pe, max_step, split_count, passed)
                for c in range(PARTS):
                    last = pe.transpose(bank[number % RING][0:n, c * P // 2:(c + 1) * P // 2].bitcast(BF16),
                                        max_parts[:, c, 0:n], m.ident_b[:, :])
                last.then_inc(job_ready, 1)

            def window(g, number, w):
                free(g, number)
                pe.wait_ge(o_out, raised(g, WINS, w + 1))
                for t in range(BT):
                    last = pe.transpose(bank[number % RING][:, t * P:(t + 1) * P], osb[:, t * P:(t + 1) * P],
                                        m.ident_f[:, :])
                last.then_inc(job_ready, 1)

            def pv(g, s, n):
                w, kb = UNITS[n]
                off = max(0, kb * P - w * WIN)
                if kb * P >= w * WIN:
                    diag = sum(1 for ww, kk in UNITS[:n + 1] if kk * P >= ww * WIN)
                    pe.wait_ge(masked, per_group(g, DIAG, diag))
                else:
                    pe.wait_ge(exp_done, raised(g, 2 * NU, 2 * n + 2))
                if kb == 0:
                    pe.wait_ge(o_out, raised(g, WINS, w))
                for h in range(GH):
                    last = pe.matmul(sums[32 * h:32 * h + 32, off:WIN], V[s][:, kb * GH + h, :],
                                     ex[n % ERING][:, h, off:WIN],
                                     start=(kb == 0), stop=(kb == (w + 1) * WIN // P - 1))
                last.then_inc(pv_done, 1)

            def step(g, s, nxt, pair):
                def job(number, what, arg):
                    if what == "chunk":
                        chunk(g, 1 - s, number, arg, pair + (1 + s))
                    elif what == "rows":
                        rows(g, number, arg, per_group(g, 10, 15 if arg else 10))
                    else:
                        window(g, number, arg)

                pe.wait_ge(rows_early, per_group(g, 16, 16))
                units = listed(nxt)
                for n, (w, kb) in enumerate(UNITS):
                    off = max(0, kb * P - w * WIN)
                    if n == first_unit[EARLY_T // BT]:
                        pe.wait_ge(rows_late, per_group(g, 16, 16))
                    todo = list(units[n])
                    for half in range(2):
                        pe.wait_ge(exp_done, raised(g, 2 * NU, 2 * n - 1 + half if n else 0))
                        for h in range(2):
                            hh = 2 * half + h
                            last = pe.matmul(score[half][:, h, off:WIN], K[s][:, kb // BT, hh, kb % BT * P:(kb % BT + 1) * P],
                                             Q[s][:, w, hh, off:WIN], start=True, stop=True)
                        last.then_inc(scores_ready, 1)
                        if todo:
                            job(*todo.pop(0))
                    if n == 0:
                        pe.wait_ge(v_laid, g + 1)
                    if n:
                        pv(g, s, n - 1)
                    while todo:
                        job(*todo.pop(0))
                pv(g, s, NU - 1)
                for j in units[NU]:
                    job(*j)

            for sem in (exp_done, o_out):
                pe.sem_inc(sem, 1)
            for number in range(BEFORE):
                if number < EARLY_JOB:
                    chunk(None, 0, number, number, 1)
                elif number > EARLY_JOB:
                    chunk(None, 0, number, number - 1, 1)
                else:
                    rows(None, number, True, 5)
            with pe.Fori(0, GROUPS // 2 - 1) as i:
                for s in range(2):
                    step(i * 2 + s, s, True, i)
            step(GROUPS - 2, 0, True, GROUPS // 2 - 1)
            step(GROUPS - 1, 1, False, GROUPS // 2 - 1)


def output(nc, m, io):
    with ExitStack() as st:
        def sb(name, shape, dt):
            return st.enter_context(nc.sbuf_tensor(f"op_{name}", shape, dt))

        rows = sb("rows", [P, 2, BT, D], F32)
        at = sb("at", [P, 2, KC, BLOCK], F32)
        wo = sb("wo", [P, KC, D], F32)
        atp = st.enter_context(nc.psum_tensor("op_atp", [P, 2, KC, BLOCK], F32))
        yp = st.enter_context(nc.psum_tensor("op_yp", [P, 2, BT, D], F32))
        w_loaded, rows_ready, atp_ready, at_ready, y_ready, x_ready = sems(
            nc, st, *(f"op_{n}" for n in ("w_loaded", "rows_ready", "atp_ready", "at_ready", "y_ready", "x_ready")))
        half = BLOCKS // BATCH
        block = st.enter_context(nc.Block())

        @block.sync
        def _(sp):
            sp.dma_start(wo[:, :, :], io["wo_t"].rearrange("(c p) f -> p c f", p=P)).then_inc(w_loaded, 16)

        @block.scalar
        def _(act):
            def gather(j):
                b, k = divmod(j, half)
                if j >= 2:
                    act.wait_ge(atp_ready, j - 1)
                src = m.AT[:, b * GH * QT:(b + 1) * GH * QT, :].rearrange("p (g t) f -> p t g f", g=GH)
                nc.scalar.activation(rows[:, j % 2, :, :].rearrange("p t (g f) -> p t g f", g=GH),
                                     src[:, k * BT:(k + 1) * BT, :, :], ACT.Copy).then_inc(rows_ready, 1)

            gather(0)
            for j in range(BLOCKS):
                if j + 1 < BLOCKS:
                    gather(j + 1)
                act.wait_ge(atp_ready, j + 1)
                if j >= 2:
                    act.wait_ge(y_ready, j - 1)
                nc.scalar.activation(at[:, j % 2, :, :], atp[:, j % 2, :, :], ACT.Copy).then_inc(at_ready, 1)

        @block.tensor
        def _(pe):
            def turn(j):
                pe.wait_ge(rows_ready, j + 1)
                if j >= 2:
                    pe.wait_ge(at_ready, j - 1)
                for c in range(KC):
                    for t in range(BT):
                        last = pe.transpose(atp[:, j % 2, c, t * P:(t + 1) * P], rows[:, j % 2, t, c * P:(c + 1) * P],
                                            m.ident_f[:, :])
                last.then_inc(atp_ready, 1)

            turn(0)
            pe.wait_ge(w_loaded, 16)
            for j in range(BLOCKS):
                if j + 1 < BLOCKS:
                    turn(j + 1)
                pe.wait_ge(at_ready, j + 1)
                if j >= 2:
                    pe.wait_ge(x_ready, j - 1)
                for t in range(BT):
                    for c in range(KC):
                        last = pe.matmul(yp[:, j % 2, t, :], at[:, j % 2, c, t * P:(t + 1) * P], wo[:, c, :],
                                         start=(c == 0), stop=(c == KC - 1))
                last.then_inc(y_ready, 1)

        @block.vector
        def _(dve):
            for j in range(BLOCKS):
                dve.wait_ge(y_ready, j + 1)
                xb = m.X[:, j * BT:(j + 1) * BT, :]
                nc.vector.tensor_tensor(xb, yp[:, j % 2, :, :], xb, ALU.add).then_inc(x_ready, 1)


def build(nc, io):
    with ExitStack() as st:
        def sb(name, shape, dt, stack=st):
            return stack.enter_context(nc.sbuf_tensor(name, shape, dt))

        def dram(name, shape, dt):
            return nc.dram_tensor(name, shape, dt, kind="Internal").ap()

        m = Core()
        m.X = sb("X", [P, TILES, D], F32)
        m.ident_f = sb("ident_f", [P, P], F32)
        m.ident_b = sb("ident_b", [P, P], BF16)
        m.ones_b = sb("ones_b", [P, P], BF16)
        m.before = sb("before", [P, P], BF16)
        m.maskneg = sb("maskneg", [P, WIN], F32)
        m.neghalf = sb("neghalf", [P, TILES], F32)
        m.rank = sb("rank", [P, TILES, EXPERTS], F32)
        m.XS = [dram(f"slots{n}", (TOKENS, ROW), F32) for n in range(2)]
        m.SUM = dram("sum", (TOKENS, D), F32)
        m.QK = [dram(n, (BLOCKS, PARTS * D, BLOCK), BF16) for n in ("q_parts", "k_parts")]
        m.VALUES = dram("values", (TILES, P, D), F32)
        m.MAXROWS = [dram("max_early", (PARTS, GH * EARLY_T, P), BF16),
                     dram("max_late", (PARTS, GH * (QT - EARLY_T), P), BF16)]
        constants(nc, m, io)
        moe(nc, m, "f0", m.XS[0], m.SUM, io, False)
        with ExitStack() as mid:
            m.Q = [sb(f"q{s}", [AROWS, WINS, GH, WIN], BF16, mid) for s in range(2)]
            m.K = [sb(f"k{s}", [AROWS, WINS, GH, WIN], BF16, mid) for s in range(2)]
            m.V = [sb(f"v{s}", [P, QT * GH, 2 * DH], F32, mid) for s in range(2)]
            m.part_max = [sb(f"pm{s}", [P, QT * GH, WINS], F32, mid) for s in range(2)]
            project(nc, m, io)
            m.AT = sb("AT", [P, GROUPS * QT, GF], F32, mid)
            attend(nc, m)
            output(nc, m, io)
        moe(nc, m, "f1", m.XS[1], io["out"], io, True)


def kernel(**inputs):
    import numpy as np
    import concourse.bacc as bacc
    from concourse.bass_utils import run_bass_kernel_spmd

    def get(name):
        return np.asarray(inputs[name])

    def by_dim(w):
        return w.T.reshape(D, HEADS // GH, GH, DH).transpose(0, 1, 3, 2).reshape(D, D)

    wkv = get("L0_attn_Wkv")
    arrays = {
        "x": get("L0_attn_x").reshape(TOKENS, D),
        "wq_t": by_dim(get("L0_attn_Wq")),
        "wk_t": by_dim(wkv[:D]),
        "wv_t": wkv[D:].T,
        "wo_t": get("L0_attn_Wo").T,
        "wg": get("L0_ffn_wg"),
        "w_t": get("L0_ffn_W").transpose(0, 2, 1),
        "b": get("L0_ffn_b"),
    }
    arrays = {n: np.ascontiguousarray(a) for n, a in arrays.items()}
    nc = bacc.Bacc("TRN2", target_bir_lowering=False, num_devices=1)
    io = {n: nc.dram_tensor(n, a.shape, mybir.dt.from_np(a.dtype), kind="ExternalInput").ap()
          for n, a in arrays.items()}
    io["out"] = nc.dram_tensor("out", (TOKENS, D), F32, kind="ExternalOutput").ap()
    build(nc, io)
    r = run_bass_kernel_spmd(nc, [arrays], core_ids=[0])
    return r.results[0]["out"].reshape(BATCH, SEQ, D)
```

```python
from contextlib import ExitStack

import concourse.bass as bass
from concourse import mybir

P = 128
BATCH, SEQ, D = 2, 2048, 256
HEADS, EXPERTS = 16, 8
DH = D // HEADS
TOKENS = BATCH * SEQ
TILES = TOKENS // P
CAP = TOKENS // EXPERTS
KC = D // P
BT = 4
BLOCK = BT * P
BLOCKS = TOKENS // BLOCK
LN_EPS = 1e-5
DEN_EPS = 1e-8
SCALE = DH ** -0.5
NEG = -3.0e38

GH = 4
GROUPS = BATCH * HEADS // GH
GF = GH * DH
PARTS = 3
ROWS = 6 * DH
AROWS = ROWS + PARTS
WIN = 512
WINS = SEQ // WIN
QT = SEQ // P
UNITS = [(w, kb) for w in range(WINS) for kb in range((w + 1) * WIN // P)]
NU = len(UNITS)
ERING = 4
CHUNKS = [(t, h, c, min(WIN, (t + 1) * P - c * WIN))
          for t in range(QT) for h in range(GH) for c in range(t // BT + 1)]
N_CHUNKS = len(CHUNKS)
EARLY_T = 12
EARLY_CHUNKS = sum(1 for c in CHUNKS if c[0] < EARLY_T)
RING = 3
AHEAD = 20
EARLY_JOB = 3
QROWS = [(0, 3, 0, False), (3, 2, 1, False), (5, 1, 2, False)]
KROWS = [(0, 3, 0, True), (3, 2, 0, True), (5, 1, 0, False)]
PROJECT_CHUNKS = [(4, 4, 4)] * 2 + [(5, 6, 7)] * 4
LAST_CHUNKS = 8
PROJECTED = EARLY_CHUNKS + LAST_CHUNKS
assert sum(sum(c) for c in PROJECT_CHUNKS) == EARLY_CHUNKS
QDMAS = len(QROWS) + len(KROWS)
ROUNDS = 4
ROW = D + 2
EMPTY = 4
FILLS = TILES // EMPTY
NOBODY = 1 << 24

ALU = mybir.AluOpType
ACT = mybir.ActivationFunctionType
AX = mybir.AxisListType
F32 = mybir.dt.float32
BF16 = mybir.dt.bfloat16
I32 = mybir.dt.int32
ds = bass.ds


class Core:
    pass


def sems(nc, stack, *names):
    return [stack.enter_context(nc.semaphore(n)) for n in names]


def wait_alone(eng, sem, value, passed):
    eng.wait_ge(sem, value)
    eng.sem_inc(passed, 1)


def fill_slots(eng, m, xs, filled):
    per = P * EMPTY
    for k in range(FILLS):
        eng.dma_start(xs[k * per:(k + 1) * per, :].rearrange("(p a) d -> p (a d)", p=P),
                      m.empty[:, :, :].rearrange("p a d -> p (a d)")).then_inc(filled, 16)


def constants(nc, m, io):
    with ExitStack() as st:
        made, zeroed, ones_made = sems(nc, st, "c_made", "c_zeroed", "c_ones")
        block = st.enter_context(nc.Block())
        per = TILES // ROUNDS

        @block.sync
        def _(sp):
            for r in range(ROUNDS):
                sp.dma_start(m.X[:, r * per:(r + 1) * per, :],
                             io["x"][r * per * P:(r + 1) * per * P, :].rearrange("(i p) d -> p i d", p=P))\
                    .then_inc(m.x_in[r], 16)
            sp.wait_ge(zeroed, 2)
            fill_slots(sp, m, m.XS[0], m.filled[0])

        @block.scalar
        def _(act):
            act.dma_start(m.wg[:, :, :], io["wg"].rearrange("(c p) e -> p c e", p=P)).then_inc(m.wg_loaded, 16)

        @block.vector
        def _(dve):
            nc.vector.memset(m.empty[:, :, 0:D], 0.0).then_inc(zeroed, 1)
            nc.vector.memset(m.empty[:, :, D:ROW].bitcast(I32), NOBODY).then_inc(zeroed, 1)
            nc.vector.memset(m.ones_b[:, :], 1.0).then_inc(ones_made, 1)
            nc.vector.memset(m.neghalf[:, :], -0.5).then_inc(ones_made, 1)

        @block.gpsimd
        def _(pool):
            nc.gpsimd.memset(m.ident_f[:, :], 0.0).then_inc(made, 1)
            nc.gpsimd.memset(m.ident_b[:, :], 0.0).then_inc(made, 1)
            nc.gpsimd.memset(m.before[:, :], 1.0).then_inc(made, 1)
            nc.gpsimd.memset(m.maskneg[:, :], 0.0).then_inc(made, 1)
            pool.wait_ge(made, 4)
            nc.gpsimd.affine_select(out=m.ident_f[:, :], in_=m.ident_f[:, :], compare_op=ALU.not_equal, fill=1.0,
                                    base=0, pattern=[[-1, P]], channel_multiplier=1).then_inc(made, 1)
            nc.gpsimd.affine_select(out=m.ident_b[:, :], in_=m.ident_b[:, :], compare_op=ALU.not_equal, fill=1.0,
                                    base=0, pattern=[[-1, P]], channel_multiplier=1).then_inc(made, 1)
            nc.gpsimd.affine_select(out=m.before[:, :], in_=m.before[:, :], compare_op=ALU.is_gt, fill=0.0,
                                    base=0, pattern=[[1, P]], channel_multiplier=-1).then_inc(made, 1)
            nc.gpsimd.affine_select(out=m.maskneg[:, :], in_=m.maskneg[:, :], compare_op=ALU.is_ge, fill=NEG,
                                    base=WIN - P, pattern=[[-1, WIN]], channel_multiplier=1).then_inc(made, 1)
            for e in range(EXPERTS):
                nc.gpsimd.memset(m.rank[:, :, e:e + 1], float(EXPERTS - e)).then_inc(made, 1)


class Moments:

    def __init__(self, nc, stack, tag, m, rounds):
        def sb(name, shape):
            return stack.enter_context(nc.sbuf_tensor(f"{tag}_{name}", shape, F32))

        self.nc, self.m, self.n = nc, m, TILES // rounds
        self.stats = sb("stats", [P, TILES, 6])
        self.work = sb("work", [P, 4, TILES])
        self.mean, self.var_eps, self.rstd = (sb(n, [P, TILES]) for n in ("mean", "var_eps", "rstd"))
        self.st_done, self.sum_done, self.step, self.var_done, self.rstd_done = sems(
            nc, stack, *(f"{tag}_{n}" for n in ("st_done", "sum_done", "mo_step", "var_done", "rstd_done")))

    def vector(self, dve, r):
        nc, at = self.nc, slice(r * self.n, (r + 1) * self.n)
        a, b, c, d = (self.work[:, n, at] for n in range(4))
        for i in range(at.start, at.stop):
            nc.vector.bn_stats(self.stats[:, i, :], self.m.X[:, i, :]).then_inc(self.st_done, 1)
        dve.wait_ge(self.st_done, at.stop)
        mean0, m20, mean1, m21 = (self.stats[:, at, n] for n in (1, 2, 4, 5))
        nc.vector.tensor_tensor(a, mean0, mean1, ALU.add).then_inc(self.sum_done, 1)
        nc.vector.tensor_tensor(b, mean0, mean1, ALU.subtract).then_inc(self.sum_done, 1)
        nc.vector.tensor_tensor(c, m20, m21, ALU.add).then_inc(self.sum_done, 1)
        dve.wait_ge(self.sum_done, 3 * r + 3)
        nc.vector.tensor_scalar(self.mean[:, at], a, 0.5, None, ALU.mult).then_inc(self.step, 1)
        nc.vector.scalar_tensor_tensor(out=d, in0=b, scalar=0.25, in1=b, op0=ALU.mult, op1=ALU.mult)\
            .then_inc(self.step, 1)
        dve.wait_ge(self.step, 3 * r + 2)
        nc.vector.scalar_tensor_tensor(out=a, in0=c, scalar=1.0 / D, in1=d, op0=ALU.mult, op1=ALU.add)\
            .then_inc(self.step, 1)
        dve.wait_ge(self.step, 3 * r + 3)
        nc.vector.tensor_scalar(self.var_eps[:, at], a, LN_EPS, None, ALU.add).then_inc(self.var_done, 1)

    def gpsimd(self, pool, r):
        at = slice(r * self.n, (r + 1) * self.n)
        pool.wait_ge(self.var_done, r + 1)
        self.nc.gpsimd.tensor_tensor(self.rstd[:, at], self.var_eps[:, at], self.m.neghalf[:, at], ALU.pow)\
            .then_inc(self.rstd_done, 1)

    def normalise(self, out, i):
        return self.nc.vector.tensor_scalar(out, self.m.X[:, ds(i, 1), :].rearrange("p o d -> p (o d)"),
                                            self.mean[:, ds(i, 1)], self.rstd[:, ds(i, 1)], ALU.subtract, ALU.mult)


def moe(nc, m, tag, layer, target, io):
    xs = m.XS[layer]
    RT = TILES // ROUNDS
    YRING = 4
    RE = RT * EXPERTS
    with ExitStack() as st:
        def sb(name, shape, dt):
            return st.enter_context(nc.sbuf_tensor(f"{tag}_{name}", shape, dt))

        def sem(*names):
            return sems(nc, st, *(f"{tag}_{n}" for n in names))

        own_moments = (ROUNDS - 1,) if layer else range(ROUNDS)
        mo = m.moments if layer else Moments(nc, st, tag, m, ROUNDS)
        rows = sb("rows", [P, TILES, ROW], F32)
        xt = sb("xt", [P, 2, 2, KC, BLOCK], F32)
        z, ez, pick, ranked, at = (sb(n, [P, ROUNDS, RT, EXPERTS], F32) for n in ("z", "ez", "pick", "ranked", "at"))
        mask = sb("mask", [P, ROUNDS, RT, EXPERTS], BF16)
        before = sb("count", [P, ROUNDS + 1, EXPERTS], F32)
        lmax, se, gate, cm, loc, keep, locc, base, slotf, drop = (
            sb(n, [P, ROUNDS, RT], F32) for n in
            ("lmax", "se", "gate", "cm", "loc", "keep", "locc", "base", "slotf", "drop"))
        slot = sb("slot", [P, TILES], I32)
        weights = sb("we", [P, EXPERTS, KC, D], F32)
        bias = sb("be", [P, EXPERTS, D], F32)
        xe = sb("xe", [P, EXPERTS, BT, ROW], F32)
        xet = sb("xet", [P, 2, KC, BLOCK], F32)
        ye = sb("ye", [P, YRING, BT, D], F32)
        xtp = st.enter_context(nc.psum_tensor(f"{tag}_xtp", [P, 2, KC, BLOCK], F32))
        pos = st.enter_context(nc.psum_tensor(f"{tag}_pos", [P, ROUNDS, P], F32))
        yp = st.enter_context(nc.psum_tensor(f"{tag}_yp", [P, 2, 2 * D], F32))
        lgp = st.enter_context(nc.psum_tensor(f"{tag}_lg", [P, 2 * D], F32))
        lg = [lgp[:, 0:RE], yp[:, 0, 0:RE]]
        (counted, numbered, xn_ready, xtp_ready, xt_ready, lg_ready, chain, z_ready, ez_ready,
         mask_ready, pos_ready, slot_ready, scattered, w_loaded, xetp_ready, xet_ready, yp_ready,
         yp_read, ye_ready) = sem(
            "counted", "numbered", "xn_ready", "xtp_ready", "xt_ready", "lg_ready", "chain", "z_ready",
            "ez_ready", "mask_ready", "pos_ready", "slot_ready", "scattered", "w_loaded",
            "xetp_ready", "xet_ready", "yp_ready", "yp_read", "ye_ready")
        xe_in = sem(*(f"xe_in{e}" for e in range(EXPERTS)))
        added = sem(*(f"added{n}" for n in range(YRING)))
        block = st.enter_context(nc.Block())

        @block.sync
        def _(sp):
            if layer == 0:
                for r in range(ROUNDS):
                    sp.wait_ge(m.x_in[r], 16)
                sp.wait_ge(m.filled[0], 16 * FILLS)
                sp.dma_start(target.rearrange("(i p) d -> p i d", p=P), m.X[:, :, :]).then_inc(m.stored[0], 16)
            sp.dma_start(weights[:, :, :, :], io["w_t"].rearrange("e (c p) f -> p e c f", p=P)).then_inc(w_loaded, 16)
            sp.dma_start(bias[:, :, :], io["b"].unsqueeze(0).to_broadcast([P, EXPERTS, D])).then_inc(w_loaded, 16)
            sp.wait_ge(scattered, 16 * TILES)

            for e in range(EXPERTS):
                sp.dma_start(xe[:, e, :, :], xs[e * CAP:(e + 1) * CAP, :].rearrange("(t p) d -> p t d", p=P))\
                    .then_inc(xe_in[e], 16)

        @block.vector
        def _(dve):
            steps = [0]

            def link(ins):
                steps[0] += 1
                ins.then_inc(chain, 1)
                dve.wait_ge(chain, steps[0])

            def normalise(r):
                dve.wait_ge(mo.rstd_done, r + 1)
                for i in range(r * RT, (r + 1) * RT):
                    mo.normalise(rows[:, i, 0:D], i).then_inc(xn_ready, 1)

            def wide(a, r):
                return a[:, r, :].unsqueeze(2).to_broadcast([P, RT, EXPERTS])

            def choose(r):
                dve.wait_ge(lg_ready, r + 1)
                logits = lg[r % 2].rearrange("p (i e) -> p i e", e=EXPERTS)
                link(nc.vector.tensor_reduce(lmax[:, r, :], logits, AX.X, ALU.max))
                nc.vector.tensor_tensor(z[:, r, :, :], logits, wide(lmax, r), ALU.subtract).then_inc(z_ready, 1)
                dve.wait_ge(z_ready, r + 1)
                link(nc.vector.tensor_scalar(pick[:, r, :, :], z[:, r, :, :], 0.0, None, ALU.is_ge))
                link(nc.vector.tensor_tensor(ranked[:, r, :, :], pick[:, r, :, :], m.rank[:, 0:RT, :], ALU.mult))
                link(nc.vector.tensor_reduce(cm[:, r, :], ranked[:, r, :, :], AX.X, ALU.max))
                nc.vector.tensor_tensor(mask[:, r, :, :], ranked[:, r, :, :], wide(cm, r), ALU.is_equal)\
                    .then_inc(mask_ready, 1)

            def place(r):
                tiles = slice(r * RT, (r + 1) * RT)
                dve.wait_ge(ez_ready, r + 1)
                link(nc.vector.tensor_reduce(se[:, r, :], ez[:, r, :, :], AX.X, ALU.add))
                link(nc.vector.reciprocal(gate[:, r, :], se[:, r, :]))
                link(nc.vector.tensor_scalar(base[:, r, :], cm[:, r, :], -float(CAP), float(CAP * EXPERTS),
                                             ALU.mult, ALU.add))
                dve.wait_ge(pos_ready, r + 1)
                dve.wait_ge(mask_ready, r + 1)
                counts = pos[:, r, 0:RE].rearrange("p (i e) -> p i e", e=EXPERTS)
                link(nc.vector.tensor_tensor(at[:, r, :, :], counts,
                                             before[:, r:r + 1, :].to_broadcast([P, RT, EXPERTS]), ALU.add))
                link(nc.vector.tensor_tensor(before[:, r + 1, :], pos[:, r, RE:RE + EXPERTS], before[:, r, :],
                                             ALU.add))
                link(nc.vector.tensor_tensor(pick[:, r, :, :], at[:, r, :, :], mask[:, r, :, :], ALU.mult))
                link(nc.vector.tensor_reduce(loc[:, r, :], pick[:, r, :, :], AX.X, ALU.add))
                link(nc.vector.tensor_scalar(keep[:, r, :], loc[:, r, :], float(CAP), None, ALU.is_lt))
                link(nc.vector.scalar_tensor_tensor(out=rows[:, tiles, D + 1], in0=gate[:, r, :], scalar=0.5,
                                                    in1=keep[:, r, :], op0=ALU.mult, op1=ALU.mult))
                link(nc.vector.tensor_tensor(slotf[:, r, :], base[:, r, :], loc[:, r, :], ALU.add))
                link(nc.vector.tensor_scalar(drop[:, r, :], keep[:, r, :], -2.0 * TOKENS, 2.0 * TOKENS,
                                             ALU.mult, ALU.add))
                nc.vector.tensor_tensor(slot[:, tiles], slotf[:, r, :], drop[:, r, :], ALU.add)\
                    .then_inc(slot_ready, 1)

            nc.vector.memset(before[:, 0, :], 0.0).then_inc(counted, 1)
            dve.wait_ge(counted, 1)
            def moments(r):
                if layer == 0 and r < ROUNDS:
                    dve.wait_ge(m.x_in[r], 16)
                if r < ROUNDS and r in own_moments:
                    mo.vector(dve, r)

            moments(0)
            normalise(0)
            moments(1)
            normalise(1)
            moments(2)
            for r in range(ROUNDS):
                choose(r)
                place(r)
                if r + 2 < ROUNDS:
                    normalise(r + 2)
                moments(r + 3)

            dve.wait_ge(w_loaded, 32)

            for e in range(EXPERTS):
                dve.wait_ge(xe_in[e], 16)
                if e >= YRING:
                    dve.wait_ge(added[e % YRING], e // YRING * (16 * BT))
                for u in range(2):
                    dve.wait_ge(yp_ready, e * 2 + (u + 1))
                    pair = ye[:, e % YRING, 2 * u:2 * u + 2, :]
                    nc.vector.tensor_tensor(pair, yp[:, u, :].rearrange("p (t d) -> p t d", d=D),
                                            bias[:, e:e + 1, :].to_broadcast([P, 2, D]), ALU.add).then_inc(yp_read, 1)
                    dve.wait_ge(yp_read, e * 2 + (u + 1))
                    for t in range(2 * u, 2 * u + 2):
                        rows_out = ye[:, e % YRING, t, :]
                        nc.vector.tensor_scalar(rows_out, rows_out, xe[:, e, t, D + 1:D + 2], None, ALU.mult)\
                            .then_inc(ye_ready, 1)

        @block.gpsimd
        def _(pool):
            nc.gpsimd.iota(rows[:, :, D].bitcast(I32), pattern=[[P, TILES]], base=0, channel_multiplier=1)\
                .then_inc(numbered, 1)
            pool.wait_ge(numbered, 1)

            def scatter(r):
                pool.wait_ge(slot_ready, r + 1)
                for i in range(r * RT, (r + 1) * RT):
                    nc.gpsimd.indirect_dma_start(
                        out=xs[:, :], out_offset=bass.IndirectOffsetOnAxis(ap=slot[:, i:i + 1], axis=0),
                        in_=rows[:, i, :], in_offset=None, bounds_check=TOKENS - 1,
                        oob_is_err=False).then_inc(scattered, 16)

            for r in range(2):
                if r in own_moments:
                    mo.gpsimd(pool, r)
            for r in range(ROUNDS):
                if r + 2 in own_moments:
                    mo.gpsimd(pool, r + 2)
                if r == 0:
                    pool.wait_ge(m.filled[layer], 16 * FILLS)
                scatter(r)
            pool.wait_ge(m.stored[layer], (16, 16 * BLOCKS)[layer])

            for e in range(EXPERTS):
                for t in range(BT):
                    pool.wait_ge(ye_ready, e * BT + t + 1)
                    nc.gpsimd.indirect_dma_start(
                        out=target, out_offset=bass.IndirectOffsetOnAxis(ap=xe[:, e, t, D:D + 1].bitcast(I32), axis=0),
                        in_=ye[:, e % YRING, t, :], in_offset=None, bounds_check=TOKENS - 1, oob_is_err=False,
                        compute_op=ALU.add).then_inc(added[e % YRING], 16)
            for n in range(YRING):
                pool.wait_ge(added[n], EXPERTS // YRING * BT * 16)

        @block.scalar
        def _(act):

            def exps(r):
                act.wait_ge(z_ready, r + 1)
                nc.scalar.activation(ez[:, r, :, :], z[:, r, :, :], ACT.Exp).then_inc(ez_ready, 1)

            for r in range(ROUNDS):
                if r:
                    exps(r - 1)
                for b in range(2):
                    act.wait_ge(xtp_ready, 2 * r + b + 1)
                    if r >= 2:
                        act.wait_ge(lg_ready, r - 1)
                    nc.scalar.activation(xt[:, r % 2, b, :, :], xtp[:, b, :, :], ACT.Copy).then_inc(xt_ready, 1)
            exps(ROUNDS - 1)

            for e in range(EXPERTS):
                act.wait_ge(xetp_ready, e + 1)
                if e >= 2:
                    act.wait_ge(yp_ready, 2 * e - 2)
                nc.scalar.activation(xet[:, e % 2, :, :], xtp[:, e % 2, :, :], ACT.Copy).then_inc(xet_ready, 1)
            if layer == 0:
                for n, name in enumerate(("wq_t", "wk_t", "wv_t")):
                    act.dma_start(m.w[:, n, :, :], io[name].rearrange("(c p) f -> p c f", p=P)).then_inc(m.w_loaded, 16)

        @block.tensor
        def _(pe):
            def turn(r):
                for b in range(2):
                    for t in range(BT):
                        i = 2 * BT * r + b * BT + t
                        if t == 0:
                            pe.wait_ge(xn_ready, i + BT)
                            if r:
                                pe.wait_ge(xt_ready, 2 * r - 1 + b)
                        for c in range(KC):
                            last = pe.transpose(xtp[:, b, c, t * P:(t + 1) * P], rows[:, i, c * P:(c + 1) * P],
                                                m.ident_f[:, :])
                    last.then_inc(xtp_ready, 1)

            def logits(r):
                for b in range(2):
                    pe.wait_ge(xt_ready, 2 * r + b + 1)
                    for t in range(BT):
                        i = b * BT + t
                        for c in range(KC):
                            last = pe.matmul(lg[r % 2][:, i * EXPERTS:(i + 1) * EXPERTS], xt[:, r % 2, b, c, t * P:(t + 1) * P],
                                             m.wg[:, c, :], start=(c == 0), stop=(c == KC - 1))
                last.then_inc(lg_ready, 1)

            def count(r):
                pe.wait_ge(mask_ready, r + 1)
                pe.matmul(pos[:, r, 0:RE], m.before[:, :], mask[:, r, :, :].rearrange("p i e -> p (i e)"),
                          start=True, stop=False)
                for i in range(RT - 1):
                    later = RT - 1 - i
                    pe.matmul(pos[:, r, (i + 1) * EXPERTS:RE].rearrange("p (i e) -> p i e", e=EXPERTS), m.ones_b[:, :],
                              mask[:, r, i:i + 1, :].to_broadcast([P, later, EXPERTS]), start=False,
                              stop=(i == RT - 2))
                for i in range(RT):
                    last = pe.matmul(pos[:, r, RE:RE + EXPERTS], m.ones_b[:, :], mask[:, r, i, :], start=(i == 0),
                                     stop=(i == RT - 1))
                last.then_inc(pos_ready, 1)

            pe.wait_ge(m.wg_loaded, 16)
            for r in range(ROUNDS):
                turn(r)
                if r:
                    count(r - 1)
                logits(r)
            count(ROUNDS - 1)

            pe.wait_ge(w_loaded, 32)
            pe.wait_ge(xt_ready, 2 * ROUNDS)

            def turn_expert(e):
                pe.wait_ge(xe_in[e], 16)
                if e >= 2:
                    pe.wait_ge(xet_ready, e - 1)
                for c in range(KC):
                    for t in range(BT):
                        last = pe.transpose(xtp[:, e % 2, c, t * P:(t + 1) * P], xe[:, e, t, c * P:(c + 1) * P],
                                            m.ident_f[:, :])
                last.then_inc(xetp_ready, 1)

            turn_expert(0)
            for e in range(EXPERTS):
                if e + 1 < EXPERTS:
                    turn_expert(e + 1)
                pe.wait_ge(xet_ready, e + 1)
                for u in range(2):
                    if e:
                        pe.wait_ge(yp_read, e * 2 + (u - 1))
                    for t in range(2 * u, 2 * u + 2):
                        for c in range(KC):
                            last = pe.matmul(yp[:, u, t % 2 * D:(t % 2 + 1) * D], xet[:, e % 2, c, t * P:(t + 1) * P],
                                             weights[:, e, c, :], start=(c == 0), stop=(c == KC - 1))
                    last.then_inc(yp_ready, 1)


def load_quarter(eng, m, b, hg, s, w):
    for buf, dram, rows in ((m.Q[s], m.QK[0], QROWS), (m.K[s], m.QK[1], KROWS)):
        for r0, n, part, successive in rows:
            src = dram[b * WINS + w, :, :].rearrange("(c g) t -> c g t", c=PARTS)[
                part:part + (n if successive else 1), ds(hg * GF, GF), :].rearrange("c (d h) t -> c d (h t)", h=GH)
            if n > 1 and not successive:
                src = src.to_broadcast([n, DH, GH * WIN])
            eng.dma_start(buf[r0 * DH:(r0 + n) * DH, w, :, :].rearrange("r h t -> r (h t)"), src)\
                .then_inc(m.quarter[s][w], 16)


def chunk_scores(pe, m, s, k, bank, visit):
    t, h, c, width = CHUNKS[k]
    w = t // BT
    if k == 0 or CHUNKS[k - 1][0] // BT != w:
        pe.wait_ge(m.quarter[s][w], visit * (16 * QDMAS))
    return pe.matmul(bank[:, 0:width], m.Q[s][0:ROWS, w, h, t % BT * P:(t % BT + 1) * P],
                     m.K[s][0:ROWS, c, h, 0:width], start=True, stop=True)


def chunk_maximum(nc, m, s, k, bank, junk):
    t, h, c, width = CHUNKS[k]
    row = (t // BT * GH + h) * BT + t % BT
    out = m.part_max[s][:, row, c:c + 1]
    if c < t // BT:
        return nc.vector.tensor_reduce(out, bank[:, 0:width], AX.X, ALU.max)
    return nc.vector.tensor_tensor_reduce(
        out=junk[:, 0:width], in0=bank[:, 0:width], in1=m.maskneg[:, WIN - width:WIN], scale=1.0, scalar=NEG,
        op0=ALU.add, op1=ALU.max, accum_out=out)


def on_diagonal(k):
    return CHUNKS[k][2] == CHUNKS[k][0] // BT


def project(nc, m, io):
    after = [(0, 0, 0)] * 2 + PROJECT_CHUNKS
    first_chunk = [sum(sum(a) for a in after[:j]) for j in range(BLOCKS)]
    with ExitStack() as st:
        def sb(name, shape, dt):
            return st.enter_context(nc.sbuf_tensor(f"pr_{name}", shape, dt))

        mo = Moments(nc, st, "pr", m, ROUNDS)
        ring = sb("ring", [P, 2, BT, D], F32)
        xt = sb("xt", [P, 2, KC, BLOCK], F32)
        w = m.w
        parts = sb("parts", [P, 2, 2, PARTS, KC * BLOCK], BF16)
        rest = sb("rest", [P, 2, 2, KC * BLOCK], F32)
        vals = sb("vals", [P, 2, BT, D], F32)
        xtp = st.enter_context(nc.psum_tensor("pr_xtp", [P, KC, BLOCK], F32))
        qkp = [st.enter_context(nc.psum_tensor(f"pr_{n}p", [P, KC * BLOCK], F32)) for n in "qk"]
        vp = qkp[0][:, :].rearrange("p (t d) -> p t d", d=D)
        bank = [st.enter_context(nc.psum_tensor(f"pr_b{r}", [P, WIN], F32)) for r in range(2)]
        junk = sb("junk", [P, 2, WIN], BF16)
        (xn_ready, xtp_ready, xt_ready, v_ready, v_out, stored0, stored1, filled) = sems(
            nc, st, *(f"pr_{n}" for n in ("xn_ready", "xtp_ready", "xt_ready", "v_ready", "v_out",
                                          "stored0", "stored1", "filled")))
        x_in = sems(nc, st, *(f"pr_x_in{r}" for r in range(ROUNDS)))
        max_ready, max_read = sems(nc, st, "pr_max_ready", "pr_max_read")
        qk_ready = sems(nc, st, "pr_q_ready", "pr_k_ready")
        part1 = sems(nc, st, "pr_q_part1", "pr_k_part1")
        rest1 = sems(nc, st, "pr_q_rest", "pr_k_rest")
        part2 = sems(nc, st, "pr_q_part2", "pr_k_part2")
        part3 = sems(nc, st, "pr_q_part3", "pr_k_part3")
        stored = (stored0, stored1)
        dmas = 3
        scale = (SCALE, 1.0)
        block = st.enter_context(nc.Block())

        @block.vector
        def _(dve):
            def normalise(j):
                if j % 2 == 0:
                    dve.wait_ge(mo.rstd_done, j // 2 + 1)
                if j >= 2:
                    dve.wait_ge(xtp_ready, j - 1)
                for t in range(BT):
                    mo.normalise(ring[:, j % 2, t, :], j * BT + t).then_inc(xn_ready, 1)

            def split(j, n):
                s = j % 2
                if j >= 2:
                    dve.wait_ge(stored[s], j // 2 * (dmas * 16))
                first, second = (parts[:, s, n, c, :] for c in range(2))
                dve.wait_ge(qk_ready[n], j + 1)
                dve.wait_ge(part1[n], j + 1)
                nc.vector.scalar_tensor_tensor(out=rest[:, s, n, :], in0=qkp[n][:, :], scalar=scale[n], in1=first,
                                               op0=ALU.mult, op1=ALU.subtract).then_inc(rest1[n], 1)
                maxima(1)
                dve.wait_ge(rest1[n], j + 1)
                nc.vector.tensor_copy(second, rest[:, s, n, :]).then_inc(part2[n], 1)

            taken = [0, 0]

            def maxima(n):
                for k in range(taken[0], min(taken[0] + n, taken[1])):
                    if k == 0:
                        dve.wait_ge(filled, 1)
                    if k >= 2 and on_diagonal(k):
                        dve.wait_ge(max_read, k - 1)
                    dve.wait_ge(max_ready, k + 1)
                    chunk_maximum(nc, m, 0, k, bank[k % 2], junk[:, k % 2, :]).then_inc(max_read, 1)
                    taken[0] += 1

            for r in range(2):
                dve.wait_ge(x_in[r], 16)
                mo.vector(dve, r)
                if r == 0:
                    normalise(0)
            normalise(1)
            for j in range(BLOCKS):
                taken[1] += sum(after[j]) + (LAST_CHUNKS if j == BLOCKS - 1 else 0)
                maxima(after[j][0] - 1)
                if j % 2 == 0 and j // 2 + 2 < ROUNDS:
                    r = j // 2 + 2
                    dve.wait_ge(x_in[r], 16)
                    mo.vector(dve, r)
                split(j, 0)
                maxima(3)
                if j + 2 < BLOCKS:
                    normalise(j + 2)
                maxima(3)
                split(j, 1)
                maxima(TOKENS)

        @block.gpsimd
        def _(pool):
            def third_parts(j):
                s = j % 2
                if j >= 2:
                    pool.wait_ge(stored[s], j // 2 * (dmas * 16))
                for n in range(2):
                    pool.wait_ge(part2[n], j + 1)
                    nc.gpsimd.tensor_tensor(parts[:, s, n, 2, :], rest[:, s, n, :], parts[:, s, n, 1, :], ALU.subtract)\
                        .then_inc(part3[n], 1)

            for r in range(2):
                mo.gpsimd(pool, r)
            fills = ([(m.part_max[0][:, :, :], NEG)] + [(m.K[s][ROWS:AROWS, :, :, :], 1.0) for s in range(2)]
                     + [(m.V[s][:, :, DH:2 * DH], 1.0) for s in range(2)] + [(m.part_max[1][:, :, :], NEG)])
            for j in range(BLOCKS):
                third_parts(j)
                if j < len(fills):
                    pool.wait_ge(part3[1], j + 1)
                    nc.gpsimd.memset(*fills[j]).then_inc(filled, 1)
                    pool.wait_ge(filled, j + 1)
                if j < 2:
                    mo.gpsimd(pool, j + 2)

        @block.scalar
        def _(act):
            def copy_turned(j):
                act.wait_ge(xtp_ready, j + 1)
                if j >= 2:
                    act.wait_ge(v_ready, j - 1)
                nc.scalar.activation(xt[:, j % 2, :, :], xtp[:, :, :], ACT.Copy).then_inc(xt_ready, 1)

            copy_turned(0)
            for j in range(BLOCKS):
                if j + 1 < BLOCKS:
                    copy_turned(j + 1)
                if j >= 2:
                    act.wait_ge(stored[j % 2], j // 2 * (dmas * 16))
                for n in range(2):
                    act.wait_ge(qk_ready[n], j + 1)
                    nc.scalar.activation(parts[:, j % 2, n, 0, :], qkp[n][:, :], ACT.Copy, scale=scale[n])\
                        .then_inc(part1[n], 1)
                act.wait_ge(v_ready, j + 1)
                nc.scalar.activation(vals[:, j % 2, :, :], vp[:, :, :], ACT.Copy).then_inc(v_out, 1)

        @block.tensor
        def _(pe):
            def turn(j):
                pe.wait_ge(xn_ready, j * BT + BT)
                for c in range(KC):
                    for t in range(BT):
                        last = pe.transpose(xtp[:, c, t * P:(t + 1) * P], ring[:, j % 2, t, c * P:(c + 1) * P],
                                            m.ident_f[:, :])
                last.then_inc(xtp_ready, 1)

            def maxima(j, place, turn, turns):
                n = after[j][place]
                k0 = first_chunk[j] + sum(after[j][:place])
                chunks(k0 + n * turn // turns, k0 + n * (turn + 1) // turns)

            def chunks(start, stop):
                for k in range(start, stop):
                    if k >= 2:
                        pe.wait_ge(max_read, k - 1)
                    chunk_scores(pe, m, 0, k, bank[k % 2], 1).then_inc(max_ready, 1)

            turn(0)
            pe.wait_ge(m.w_loaded, 16 * 3)
            for j in range(BLOCKS):
                s = j % 2
                pe.wait_ge(xt_ready, j + 1)
                if j + 1 < BLOCKS:
                    turn(j + 1)
                for n in range(2):
                    if j and n == 0:
                        pe.wait_ge(v_out, j)
                    elif j:
                        pe.wait_ge(rest1[n], j)
                    for co in range(KC):
                        for c in range(KC):
                            last = pe.matmul(qkp[n][:, co * BLOCK:(co + 1) * BLOCK], w[:, n, c, co * P:(co + 1) * P],
                                             xt[:, s, c, :], start=(c == 0), stop=(c == KC - 1))
                            if (co, c) == (KC - 1, KC - 1):
                                last.then_inc(qk_ready[n], 1)
                            maxima(j, n, co * KC + c, KC * KC)
                pe.wait_ge(rest1[0], j + 1)
                for t in range(BT):
                    for c in range(KC):
                        last = pe.matmul(vp[:, t, :], xt[:, s, c, t * P:(t + 1) * P], w[:, 2, c, :],
                                         start=(c == 0), stop=(c == KC - 1))
                    if t == BT - 1:
                        last.then_inc(v_ready, 1)
                    maxima(j, 2, t, BT)
            chunks(EARLY_CHUNKS, PROJECTED)

        @block.sync
        def _(sp):
            per = TOKENS // ROUNDS
            for r in range(ROUNDS):
                sp.dma_start(m.X[:, r * TILES // ROUNDS:(r + 1) * TILES // ROUNDS, :],
                             m.SUM[r * per:(r + 1) * per, :].rearrange("(i p) d -> p i d", p=P)).then_inc(x_in[r], 16)
            for j in range(BLOCKS):
                s = j % 2
                for n in range(2):
                    sp.wait_ge(part3[n], j + 1)
                    sp.dma_start(m.QK[n][j, :, :].rearrange("(x p) t -> p x t", p=P),
                                 parts[:, s, n, :, :].rearrange("p a (c t) -> p (a c) t", c=KC))\
                        .then_inc(stored[s], 16)
                sp.wait_ge(v_out, j + 1)
                sp.dma_start(m.VALUES[j * BT:(j + 1) * BT, :, :].rearrange("t p f -> p t f"), vals[:, s, :, :])\
                    .then_inc(stored[s], 16)
                if j < WINS:
                    sp.wait_ge(stored[s], (j // 2 + 1) * (dmas * 16))
                    load_quarter(sp, m, 0, 0, 0, j)
            for s in range(2):
                sp.wait_ge(stored[s], BLOCKS // 2 * dmas * 16)


def attend(nc, m):
    with ExitStack() as st:
        def sb(name, shape, dt):
            return st.enter_context(nc.sbuf_tensor(f"at_{name}", shape, dt))

        def ps(name, shape, dt=F32):
            return st.enter_context(nc.psum_tensor(f"at_{name}", shape, dt))

        Q, K, V, part_max = m.Q, m.K, m.V, m.part_max
        v_raw = sb("vr", [P, QT, GF], F32)
        ex = [sb(f"e{r}", [P, GH, WIN], F32) for r in range(ERING)]
        neg_max = sb("nm", [P, GH * QT], F32)
        left = sb("left", [P, GH * QT], F32)
        max_parts = sb("mp", [P, PARTS, GH * QT], BF16)
        max_rows = sb("mr", [GH * EARLY_T, PARTS, P], BF16)
        junk = sb("junk", [P, RING, WIN], BF16)
        osb = sb("osb", [P, WIN], F32)
        den = sb("den", [P, 2, BT * GH], F32)
        score = [ps(f"s{h}", [P, 2, WIN]) for h in range(2)]
        bank = [ps(f"b{r}", [P, WIN]) for r in range(RING)]
        sums = ps("o", [P, WIN])

        (scores_ready, exp_done, pv_done, masked, job_ready, job_read, max_step, rows_ready, rows_stored, rows_early,
         rows_late, o_out, norm_step, v_in, v_laid, passed) = sems(nc, st, *(f"at_{n}" for n in (
             "scores_ready", "exp_done", "pv_done", "masked", "job_ready", "job_read", "max_step", "rows_ready",
             "rows_stored", "rows_early", "rows_late", "o_out", "norm_step", "v_in", "v_laid", "passed")))
        block = st.enter_context(nc.Block())

        DIAG = sum(1 for w, kb in UNITS if kb * P >= w * WIN)
        first_unit = [n for n, (w, kb) in enumerate(UNITS) if kb == 0]

        def share(costs):
            return [sum(costs[:k + 1]) / sum(costs) for k in range(len(costs))]

        stream = ([("own", k) for k in range(EARLY_CHUNKS + AHEAD, N_CHUNKS)] + [("next", k) for k in range(EARLY_CHUNKS + AHEAD)])
        unit_end = share([96 + min(WIN, (w + 1) * WIN - kb * P) for w, kb in UNITS])
        jobs = [[] for _ in range(NU)]
        for job, end in zip(stream, share([64 + CHUNKS[k][3] for _, k in stream])):
            jobs[next(n for n in range(NU) if unit_end[n] >= end - 1e-9)].append(job)

        def unit_of(job):
            return next(n for n in range(NU) if job in jobs[n])

        SPLIT_LATE, SPLIT_EARLY = unit_of(("own", N_CHUNKS - 1)), unit_of(("next", EARLY_CHUNKS - 1))
        jobs[SPLIT_LATE + 2].insert(2, ("rows", False))
        jobs[SPLIT_EARLY + 2].insert(2, ("rows", True))
        for w in range(-1, WINS - 1):
            jobs[first_unit[w + 1] + 3].append(("window", w))
        PER_GROUP = sum(len(u) for u in jobs)
        BEFORE = EARLY_CHUNKS + AHEAD - PROJECTED + 1

        def listed(nxt):
            number, out = 0, []
            for unit in jobs:
                kept = [j for j in unit if nxt or j[0] in ("own", "window") or j == ("rows", False)]
                out.append([(number + k, *j) for k, j in enumerate(kept)])
                number += len(kept)
            return out

        def number_of(nxt, what):
            return next(j[0] for u in listed(nxt) for j in u if j[1:] == what)

        def raised(g, per, plus=0):
            if isinstance(g, int) and g == 0:
                plus = max(plus, 0)
            return g * per + (plus + 1)

        def per_group(g, per, plus=0):
            return g * per + plus

        def jobs_done(g, number):
            return number if g is None else g * PER_GROUP + (BEFORE + number)

        def last_use(g, number):
            if number >= RING:
                return jobs_done(g, number - RING + 1)
            if g is None:
                return None
            before = BEFORE if isinstance(g, int) and g == 0 else PER_GROUP
            return jobs_done(g, max(m for m in range(before) if m % RING == number) - before + 1)

        def groups(eng, body):
            body(0, 0, True)
            with eng.Fori(0, GROUPS // 2 - 1) as i:
                for s in (1, 0):
                    body(i * 2 + (2 - s), s, True)
            body(GROUPS - 1, 1, False)

        LAST = sum(len(u) for u in listed(False))

        def first(g):
            return isinstance(g, int) and g == 0

        @block.sync
        def _(sp):
            def load(b, hg, s, earlier):
                if earlier is not None:
                    for w in range(WINS):
                        load_quarter(sp, m, b, hg, s, w)
                if earlier is not None:
                    sp.wait_ge(v_laid, earlier)
                sp.dma_start(v_raw[:, :, :], m.VALUES[b * QT:(b + 1) * QT, :, ds(hg * GF, GF)]
                             .rearrange("k p f -> p k f")).then_inc(v_in, 16)

            def max_rows_in(g, s, early):
                w0, w1 = (0, EARLY_T // BT) if early else (EARLY_T // BT, WINS)
                dram = m.MAXROWS[0 if early else 1]
                done = per_group(g, 2, 1 if early else 2)
                if not isinstance(g, int) or g:
                    wait_alone(sp, rows_early if early else rows_late, per_group(g, 16), passed)
                wait_alone(sp, rows_ready, done, passed)
                sp.dma_start(dram.rearrange("c r x -> r c x"), max_rows[0:(w1 - w0) * GH * BT, :, :])\
                    .then_inc(rows_stored, 16)
                sp.wait_ge(rows_stored, done * 16)
                sp.dma_start(Q[s][ROWS:AROWS, w0:w1, :, :].rearrange("c w h t -> c (w h t)"),
                             dram.rearrange("c r x -> c (r x)")).then_inc(rows_early if early else rows_late, 16)

            def step(g, s, nxt, nb=None, nh=None):
                max_rows_in(g, s, False)
                if nxt:
                    max_rows_in(g + 1, 1 - s, True)
                if nb is not None:
                    sp.wait_ge(pv_done, raised(g, NU, NU))
                    load(nb, nh, s, g + 2)

            load(0, 0, 0, None)
            max_rows_in(0, 0, True)
            load(0, 1, 1, 1)
            fill_slots(sp, m, m.XS[1], m.filled[1])
            step(0, 0, True, 0, 2)
            step(1, 1, True, 0, 3)
            with sp.Fori(1, GROUPS // 2 - 1) as i:
                for s in range(2):
                    step(i * 2 + s, s, True, 1, i * 2 - 2 + s)
            step(GROUPS - 2, 0, True)
            step(GROUPS - 1, 1, False)

        @block.gpsimd
        def _(pool):
            def lay_values(g, s):
                wait_alone(pool, v_in, per_group(g, 16, 16), passed)
                nc.gpsimd.tensor_copy(V[s][:, :, 0:DH], v_raw[:, :, :].rearrange("p k (h d) -> p (k h) d", d=DH))\
                    .then_inc(v_laid, 1)

            def step(g, s, nxt):
                for n, (w, kb) in enumerate(UNITS):
                    off = kb * P - w * WIN
                    if nxt and n == NU // 2:
                        lay_values(g + 1, 1 - s)
                    if off < 0:
                        continue
                    for half in range(2):
                        wait_alone(pool, exp_done, raised(g, 2 * NU, 2 * n + half + 1), passed)
                        tri = ex[n % ERING][:, 2 * half:2 * half + 2, off:off + P]
                        nc.gpsimd.affine_select(out=tri, in_=tri, compare_op=ALU.is_ge, fill=0.0, base=0,
                                                pattern=[[0, GH // 2], [1, P]], channel_multiplier=-1)\
                            .then_inc(masked, 1)

            lay_values(0, 0)
            groups(pool, step)

        @block.scalar
        def _(act):
            def window_out(g, w, job):
                act.wait_ge(pv_done, raised(g, NU, first_unit[w + 1] if w < WINS - 1 else NU))
                if job is not None:
                    act.wait_ge(job_ready, job)
                nc.scalar.activation(osb[:, :], sums[:, :], ACT.Copy).then_inc(o_out, 1)

            def step(g, s, nxt):
                def turned(w):
                    return jobs_done(g, number_of(nxt, ("window", w - 1)) + 1)

                for n, (w, kb) in enumerate(UNITS):
                    off = max(0, kb * P - w * WIN)
                    act.wait_ge(pv_done, raised(g, NU, n - ERING + 1))
                    for half in range(2):
                        act.wait_ge(scores_ready, per_group(g, 2 * NU, 2 * n + half + 1))
                        nc.scalar.activation(ex[n % ERING][:, 2 * half:2 * half + 2, off:WIN],
                                             score[half][:, :, off:WIN], ACT.Exp).then_inc(exp_done, 1)
                    if n == 0 and not first(g):
                        window_out(g - 1, WINS - 1, jobs_done(g, number_of(True, ("window", WINS - 2)) + 1 - PER_GROUP))
                    if w > 0 and kb == 0:
                        window_out(g, w - 1, None if w == 1 and first(g) else turned(w - 1))
                if not nxt:
                    window_out(g, WINS - 1, turned(WINS - 1))

            act.sem_inc(pv_done, 1)
            groups(act, step)

        @block.vector
        def _(dve):
            def chunk(g, s, number, k):
                if on_diagonal(k):
                    if last_use(g, number) is not None:
                        dve.wait_ge(job_read, last_use(g, number))
                    wait_alone(dve, job_ready, jobs_done(g, number + 1), passed)
                else:
                    dve.wait_ge(job_ready, jobs_done(g, number + 1))
                chunk_maximum(nc, m, s, k, bank[number % RING], junk[:, number % RING, :]).then_inc(job_read, 1)

            def split(g, s, early, step, read, turned):
                r0, r1 = (0, EARLY_T * GH) if early else (EARLY_T * GH, QT * GH)
                n = r1 - r0
                top, rest = neg_max[:, 0:n], left[:, 0:n]
                one, two, three = (max_parts[:, c, 0:n] for c in range(PARTS))
                if step:
                    dve.wait_ge(max_step, per_group(g, 2 * 5, (0 if early else 5) + step))
                elif read is not None:
                    dve.wait_ge(job_read, read)
                if step == 0:
                    ins = nc.vector.tensor_reduce(top, part_max[s][:, r0:r1, :], AX.X, ALU.max, negate=True)
                elif step == 1:
                    if turned is not None:
                        dve.wait_ge(job_ready, turned)
                    ins = nc.vector.tensor_copy(one, top)
                elif step == 2:
                    ins = nc.vector.tensor_tensor(rest, top, one, ALU.subtract)
                elif step == 3:
                    ins = nc.vector.tensor_copy(two, rest)
                else:
                    ins = nc.vector.tensor_tensor(three, rest, two, ALU.subtract)
                ins.then_inc(max_step, 1)

            def rows_out(g, number, early):
                n = GH * (EARLY_T if early else QT - EARLY_T)
                dve.wait_ge(job_ready, jobs_done(g, number + 1))
                if g is not None:
                    dve.wait_ge(rows_stored, per_group(g, 32, 32 if early else 16))
                nc.vector.tensor_copy(max_rows[0:n, :, :], bank[number % RING][0:n, 0:PARTS * P // 2].bitcast(BF16)
                                      .rearrange("r (c x) -> r c x", c=PARTS)).then_inc(rows_ready, 1)
                dve.wait_ge(rows_ready, 1 if g is None else per_group(g, 2, 3 if early else 2))
                dve.sem_inc(job_read, 1)

            def normalise(at, g, number, w):
                dve.wait_ge(job_ready, jobs_done(at, number + 1))
                start = per_group(g, 2 * WINS, 2 * w)
                view = bank[number % RING][:, :].rearrange("p (t h a f) -> p (t h) a f", t=BT, h=GH, a=2)
                nc.vector.tensor_scalar(den[:, 0, :], view[:, :, 1, 0:1].rearrange("p n f -> p (n f)"), DEN_EPS, None,
                                        ALU.add).then_inc(norm_step, 1)
                dve.wait_ge(norm_step, start + 1)
                nc.vector.reciprocal(den[:, 1, :], den[:, 0, :]).then_inc(norm_step, 1)
                dve.wait_ge(norm_step, start + 2)
                nc.vector.tensor_tensor(
                    m.AT[:, ds(g * QT + w * BT, BT), :].rearrange("p t (h d) -> p (t h) d", h=GH), view[:, :, 0, :],
                    den[:, 1, :].unsqueeze(2).to_broadcast([P, BT * GH, DH]), ALU.mult).then_inc(job_read, 1)

            def null_job(number):
                dve.wait_ge(job_ready, jobs_done(0, number + 1))
                dve.wait_ge(job_read, jobs_done(0, number))
                dve.sem_inc(job_read, 1)

            def step(g, s, nxt):
                def split_between(n, step):
                    if n == SPLIT_LATE + 1:
                        split(g, s, False, step, jobs_done(g, number_of(nxt, ("own", N_CHUNKS - 1)) + 1), jobs_done(g, 0))
                    if nxt and n == SPLIT_EARLY + 1:
                        split(g + 1, 1 - s, True, step, jobs_done(g, number_of(nxt, ("next", EARLY_CHUNKS - 1)) + 1),
                              jobs_done(g, number_of(nxt, ("rows", False)) + 1))

                for n, unit in enumerate(listed(nxt)):
                    for k, (number, what, arg) in enumerate(unit):
                        if k < 5:
                            split_between(n, k)
                        if what == "own":
                            chunk(g, s, number, arg)
                        elif what == "next":
                            chunk(g, 1 - s, number, arg)
                        elif what == "rows":
                            rows_out(g, number, arg)
                        elif arg >= 0:
                            normalise(g, g, number, arg)
                        elif first(g):
                            null_job(number)
                        else:
                            normalise(g, g - 1, number, WINS - 1)
                    for k in range(len(unit), 5):
                        split_between(n, k)

            for k in range(5):
                split(0, 0, True, k, None, None)
            for number in range(BEFORE):
                if number == EARLY_JOB:
                    rows_out(None, number, True)
                else:
                    chunk(None, 0, number, PROJECTED + number - (number > EARLY_JOB))
            groups(dve, step)
            normalise(GROUPS - 1, GROUPS - 1, LAST, WINS - 1)

        @block.tensor
        def _(pe):
            def free(g, number):
                if last_use(g, number) is not None:
                    pe.wait_ge(job_read, last_use(g, number))

            def chunk(g, s, number, k, visit):
                free(g, number)
                chunk_scores(pe, m, s, k, bank[number % RING], visit).then_inc(job_ready, 1)

            def rows(g, number, early, split_count):
                n = GH * (EARLY_T if early else QT - EARLY_T)
                free(g, number)
                wait_alone(pe, max_step, split_count, passed)
                for c in range(PARTS):
                    last = pe.transpose(bank[number % RING][0:n, c * P // 2:(c + 1) * P // 2].bitcast(BF16),
                                        max_parts[:, c, 0:n], m.ident_b[:, :])
                last.then_inc(job_ready, 1)

            def window(at, g, number, w):
                free(at, number)
                pe.wait_ge(o_out, raised(g, WINS, w + 1))
                for t in range(BT):
                    last = pe.transpose(bank[number % RING][:, t * P:(t + 1) * P], osb[:, t * P:(t + 1) * P],
                                        m.ident_f[:, :])
                last.then_inc(job_ready, 1)

            def pv(g, s, n):
                w, kb = UNITS[n]
                off = max(0, kb * P - w * WIN)
                if kb == 0:
                    pe.wait_ge(o_out, raised(g, WINS, w))
                for h in range(GH):
                    half = h // 2
                    if h % 2 == 0 and kb * P >= w * WIN:
                        diag = sum(1 for ww, kk in UNITS[:n] if kk * P >= ww * WIN)
                        pe.wait_ge(masked, per_group(g, 2 * DIAG, 2 * diag + half + 1))
                    elif h % 2 == 0:
                        pe.wait_ge(exp_done, raised(g, 2 * NU, 2 * n + half + 1))
                    last = pe.matmul(sums[32 * h:32 * h + 32, off:WIN], V[s][:, kb * GH + h, :],
                                     ex[n % ERING][:, h, off:WIN],
                                     start=(kb == 0), stop=(kb == (w + 1) * WIN // P - 1))
                last.then_inc(pv_done, 1)

            def null_job(number):
                pe.wait_ge(job_read, jobs_done(0, number))
                pe.sem_inc(job_ready, 1)

            def step(g, s, nxt, visit, next_visit):
                def job(number, what, arg):
                    if what == "own":
                        chunk(g, s, number, arg, visit)
                    elif what == "next":
                        chunk(g, 1 - s, number, arg, next_visit)
                    elif what == "rows":
                        rows(g, number, arg, per_group(g, 10, 15 if arg else 10))
                    elif arg >= 0:
                        window(g, g, number, arg)
                    elif first(g):
                        null_job(number)
                    else:
                        window(g, g - 1, number, WINS - 1)

                pe.wait_ge(rows_early, per_group(g, 16, 16))
                for n, (w, kb) in enumerate(UNITS):
                    off = max(0, kb * P - w * WIN)
                    if n == first_unit[EARLY_T // BT]:
                        pe.wait_ge(rows_late, per_group(g, 16, 16))
                    todo = list(listed(nxt)[n])
                    for half in range(2):
                        pe.wait_ge(exp_done, raised(g, 2 * NU, 2 * n - 1 + half))
                        for h in range(2):
                            hh = 2 * half + h
                            last = pe.matmul(score[half][:, h, off:WIN], K[s][:, kb // BT, hh, kb % BT * P:(kb % BT + 1) * P],
                                             Q[s][:, w, hh, off:WIN], start=True, stop=True)
                        last.then_inc(scores_ready, 1)
                        if todo:
                            job(*todo.pop(0))
                    if n == 1:
                        pe.wait_ge(v_laid, g + 1)
                    if n:
                        pv(g, s, n - 1)
                    elif not first(g):
                        pv(g - 1, 1 - s, NU - 1)
                    while todo:
                        job(*todo.pop(0))

            for sem in (exp_done, o_out):
                pe.sem_inc(sem, 1)
            for number in range(BEFORE):
                if number == EARLY_JOB:
                    rows(None, number, True, 5)
                else:
                    chunk(None, 0, number, PROJECTED + number - (number > EARLY_JOB), 1)
            step(0, 0, True, 1, 1)
            with pe.Fori(0, GROUPS // 2 - 1) as i:
                step(i * 2 + 1, 1, True, i + 1, i + 2)
                step(i * 2 + 2, 0, True, i + 2, i + 2)
            step(GROUPS - 1, 1, False, GROUPS // 2, None)
            pv(GROUPS - 1, 1, NU - 1)
            window(GROUPS - 1, GROUPS - 1, LAST, WINS - 1)


def output(nc, m, io):
    with ExitStack() as st:
        def sb(name, shape, dt):
            return st.enter_context(nc.sbuf_tensor(f"op_{name}", shape, dt))

        rows = sb("rows", [P, 2, BT, D], F32)
        at = sb("at", [P, 2, KC, BLOCK], F32)
        wo = sb("wo", [P, KC, D], F32)
        atp = st.enter_context(nc.psum_tensor("op_atp", [P, 2, KC, BLOCK], F32))
        yp = st.enter_context(nc.psum_tensor("op_yp", [P, 2, BT, D], F32))
        w_loaded, rows_ready, atp_ready, at_ready, y_ready, x_ready = sems(
            nc, st, *(f"op_{n}" for n in ("w_loaded", "rows_ready", "atp_ready", "at_ready", "y_ready", "x_ready")))
        half = BLOCKS // BATCH
        block = st.enter_context(nc.Block())

        @block.sync
        def _(sp):
            sp.dma_start(wo[:, :, :], io["wo_t"].rearrange("(c p) f -> p c f", p=P)).then_inc(w_loaded, 16)
            out = io["out"].rearrange("(i p) d -> p i d", p=P)
            for j in range(BLOCKS):
                sp.wait_ge(x_ready, j + 1)
                sp.dma_start(out[:, j * BT:(j + 1) * BT, :], m.X[:, j * BT:(j + 1) * BT, :])\
                    .then_inc(m.stored[1], 16)

        @block.scalar
        def _(act):
            def gather(j):
                b, k = divmod(j, half)
                if j >= 2:
                    act.wait_ge(atp_ready, j - 1)
                src = m.AT[:, b * GH * QT:(b + 1) * GH * QT, :].rearrange("p (g t) f -> p t g f", g=GH)
                nc.scalar.activation(rows[:, j % 2, :, :].rearrange("p t (g f) -> p t g f", g=GH),
                                     src[:, k * BT:(k + 1) * BT, :, :], ACT.Copy).then_inc(rows_ready, 1)

            gather(0)
            for j in range(BLOCKS):
                if j + 1 < BLOCKS:
                    gather(j + 1)
                act.wait_ge(atp_ready, j + 1)
                if j >= 2:
                    act.wait_ge(y_ready, j - 1)
                nc.scalar.activation(at[:, j % 2, :, :], atp[:, j % 2, :, :], ACT.Copy).then_inc(at_ready, 1)

        @block.tensor
        def _(pe):
            def turn(j):
                pe.wait_ge(rows_ready, j + 1)
                if j >= 2:
                    pe.wait_ge(at_ready, j - 1)
                for c in range(KC):
                    for t in range(BT):
                        last = pe.transpose(atp[:, j % 2, c, t * P:(t + 1) * P], rows[:, j % 2, t, c * P:(c + 1) * P],
                                            m.ident_f[:, :])
                last.then_inc(atp_ready, 1)

            turn(0)
            pe.wait_ge(w_loaded, 16)
            for j in range(BLOCKS):
                if j + 1 < BLOCKS:
                    turn(j + 1)
                pe.wait_ge(at_ready, j + 1)
                if j >= 2:
                    pe.wait_ge(x_ready, j - 1)
                for t in range(BT):
                    for c in range(KC):
                        last = pe.matmul(yp[:, j % 2, t, :], at[:, j % 2, c, t * P:(t + 1) * P], wo[:, c, :],
                                         start=(c == 0), stop=(c == KC - 1))
                last.then_inc(y_ready, 1)

        @block.vector
        def _(dve):
            for j in range(BLOCKS):
                dve.wait_ge(y_ready, j + 1)
                xb = m.X[:, j * BT:(j + 1) * BT, :]
                nc.vector.tensor_tensor(xb, yp[:, j % 2, :, :], xb, ALU.add).then_inc(x_ready, 1)
                if j % 2 and j < BLOCKS - 1:
                    dve.wait_ge(x_ready, j + 1)
                    m.moments.vector(dve, j // 2)

        @block.gpsimd
        def _(pool):
            for r in range(ROUNDS - 1):
                m.moments.gpsimd(pool, r)


def build(nc, io):
    with ExitStack() as st:
        def sb(name, shape, dt, stack=st):
            return stack.enter_context(nc.sbuf_tensor(name, shape, dt))

        def dram(name, shape, dt):
            return nc.dram_tensor(name, shape, dt, kind="Internal").ap()

        m = Core()
        m.X = sb("X", [P, TILES, D], F32)
        m.ident_f = sb("ident_f", [P, P], F32)
        m.ident_b = sb("ident_b", [P, P], BF16)
        m.ones_b = sb("ones_b", [P, P], BF16)
        m.before = sb("before", [P, P], BF16)
        m.maskneg = sb("maskneg", [P, WIN], F32)
        m.neghalf = sb("neghalf", [P, TILES], F32)
        m.rank = sb("rank", [P, TILES, EXPERTS], F32)
        m.XS = [dram(f"slots{n}", (TOKENS, ROW), F32) for n in range(2)]
        m.SUM = dram("sum", (TOKENS, D), F32)
        m.QK = [dram(n, (BLOCKS, PARTS * D, BLOCK), BF16) for n in ("q_parts", "k_parts")]
        m.VALUES = dram("values", (TILES, P, D), F32)
        m.MAXROWS = [dram("max_early", (PARTS, GH * EARLY_T, P), BF16),
                     dram("max_late", (PARTS, GH * (QT - EARLY_T), P), BF16)]
        m.x_in = sems(nc, st, *(f"x_in{r}" for r in range(ROUNDS)))
        m.wg = sb("router", [P, KC, EXPERTS], F32)
        m.stored = sems(nc, st, "stored_sum", "stored_out")
        m.w = sb("w", [P, 3, KC, D], F32)
        m.wg_loaded, m.w_loaded = sems(nc, st, "wg_loaded", "w_loaded")
        m.filled = sems(nc, st, "filled0", "filled1")
        m.empty = sb("empty", [P, EMPTY, ROW], F32)
        constants(nc, m, io)
        moe(nc, m, "f0", 0, m.SUM, io)
        m.moments = Moments(nc, st, "f1", m, ROUNDS)
        with ExitStack() as mid:
            m.Q = [sb(f"q{s}", [AROWS, WINS, GH, WIN], BF16, mid) for s in range(2)]
            m.K = [sb(f"k{s}", [AROWS, WINS, GH, WIN], BF16, mid) for s in range(2)]
            m.V = [sb(f"v{s}", [P, QT * GH, 2 * DH], F32, mid) for s in range(2)]
            m.quarter = [sems(nc, mid, *(f"quarter{s}_{w}" for w in range(WINS))) for s in range(2)]
            m.part_max = [sb(f"pm{s}", [P, QT * GH, WINS], F32, mid) for s in range(2)]
            project(nc, m, io)
            m.AT = sb("AT", [P, GROUPS * QT, GF], F32, mid)
            attend(nc, m)
            output(nc, m, io)
        moe(nc, m, "f1", 1, io["out"], io)


def kernel(**inputs):
    import numpy as np
    import concourse.bacc as bacc
    from concourse.bass_utils import run_bass_kernel_spmd

    def get(name):
        return np.asarray(inputs[name])

    def by_dim(w):
        return w.T.reshape(D, HEADS // GH, GH, DH).transpose(0, 1, 3, 2).reshape(D, D)

    wkv = get("L0_attn_Wkv")
    arrays = {
        "x": get("L0_attn_x").reshape(TOKENS, D),
        "wq_t": by_dim(get("L0_attn_Wq")),
        "wk_t": by_dim(wkv[:D]),
        "wv_t": wkv[D:].T,
        "wo_t": get("L0_attn_Wo").T,
        "wg": get("L0_ffn_wg"),
        "w_t": get("L0_ffn_W").transpose(0, 2, 1),
        "b": get("L0_ffn_b"),
    }
    arrays = {n: np.ascontiguousarray(a) for n, a in arrays.items()}
    nc = bacc.Bacc("TRN2", target_bir_lowering=False, num_devices=1)
    io = {n: nc.dram_tensor(n, a.shape, mybir.dt.from_np(a.dtype), kind="ExternalInput").ap()
          for n, a in arrays.items()}
    io["out"] = nc.dram_tensor("out", (TOKENS, D), F32, kind="ExternalOutput").ap()
    build(nc, io)
    r = run_bass_kernel_spmd(nc, [arrays], core_ids=[0])
    return r.results[0]["out"].reshape(BATCH, SEQ, D)
```
